# Optimizing a Trainium2 kernel written in Bass

```python
import numpy as np
import jax
import jax.numpy as jnp

def _softmax(x, axis=-1):
    return jax.nn.softmax(x, axis=axis)

def _gelu(x):
    return jax.nn.gelu(x, approximate=True)

def _silu(x):
    return jax.nn.silu(x)

def _sigmoid(x):
    return jax.nn.sigmoid(x)

def _layernorm(x, axis=-1, eps=1e-05):
    m = jnp.mean(x, axis=axis, keepdims=True)
    v = jnp.var(x, axis=axis, keepdims=True)
    return (x - m) / jnp.sqrt(v + eps)

def _scatter_add(tgt, idx, src, axis=0):
    return tgt.at[idx].add(src)

def _segment_sum(src, seg, n):
    return jax.ops.segment_sum(src, seg, n)
kernel_name = 'mk_conv_attn_hybrid_d2_conv_nchw128_r4_a0959e'

def setup_inputs(seed: int=0):
    np.random.seed(seed)
    _w = jnp.asarray

    def _rec_inputs():
        import jax
        import jax.numpy as jnp
        _gk = jax.random.key(seed)
        x = -0.0002422 + 1 * jax.random.normal(jax.random.fold_in(_gk, 1), (32, 32, 16, 25), jnp.float32)
        return x
    x = _rec_inputs()

    def _L0_conv_setup():
        import jax, jax.numpy as jnp
        import numpy as np
        B, CIN, COUT, T, V = (32, 32, 32, 16, 25)
        CB = COUT // 4
        K = 5
        EPS = 1e-05

        def _bn(x, p):
            g, b, m, v = (p[0], p[1], p[2], p[3])
            s = g / jnp.sqrt(v + EPS)
            return x * s[None, :, None, None] + (b - m * s)[None, :, None, None]

        def _c1x1(x, W):
            return jnp.einsum('oc,bctv->botv', W, x)

        def _tconv(x, W, d):
            return jax.lax.conv_general_dilated(x, W[:, :, :, None], window_strides=(1, 1), padding=((2 * d, 2 * d), (0, 0)), rhs_dilation=(d, 1), dimension_numbers=('NCHW', 'OIHW', 'NCHW'))
        key = jax.random.key(seed)
        ks = iter(jax.random.split(key, 40))

        def adj(k):
            r = jax.random.uniform(k, (V, V))
            a = jnp.minimum(((r < 0.12) | (r.T < 0.12)).astype(jnp.float32) + jnp.eye(V, dtype=jnp.float32), 1.0)
            return a / jnp.maximum(a.sum(axis=1, keepdims=True), 1e-06)

        def bnp(k, c):
            k1, k2, k3, k4 = jax.random.split(k, 4)
            return jnp.stack([1.0 + 0.1 * jax.random.normal(k1, (c,)), 0.1 * jax.random.normal(k2, (c,)), 0.1 * jax.random.normal(k3, (c,)), jax.random.uniform(k4, (c,), minval=0.5, maxval=1.5)])

        def w(k, shape, fan_in):
            return jax.random.normal(k, shape) * (1.0 / np.sqrt(fan_in))
        inp = {'x': jax.random.normal(next(ks), (B, CIN, T, V), dtype=jnp.float32), 'A_learned': jax.random.normal(next(ks), (V, V), dtype=jnp.float32), 'A_flat': adj(next(ks)), 'A_intra': adj(next(ks)), 'A_inter': adj(next(ks)), 'Wgc': w(next(ks), (COUT, CIN), CIN), 'bn_gc': bnp(next(ks), COUT), 'Wb1': w(next(ks), (CB, COUT), COUT), 'bn_b1': bnp(next(ks), CB), 'Wt1': w(next(ks), (CB, CB, K), CB * K), 'bn_t1': bnp(next(ks), CB), 'Wb2': w(next(ks), (CB, COUT), COUT), 'bn_b2': bnp(next(ks), CB), 'Wt2': w(next(ks), (CB, CB, K), CB * K), 'bn_t2': bnp(next(ks), CB), 'Wb3': w(next(ks), (CB, COUT), COUT), 'bn_b3': bnp(next(ks), CB), 'bn_p3': bnp(next(ks), CB), 'Wb4': w(next(ks), (CB, COUT), COUT), 'bn_b4': bnp(next(ks), CB)}
        return inp
    _L0_conv_all = _L0_conv_setup()
    _L0_conv_in = {k: v for k, v in _L0_conv_all.items() if k in ('A_learned', 'A_flat', 'A_intra', 'A_inter', 'Wgc', 'bn_gc', 'Wb1', 'bn_b1', 'Wt1', 'bn_t1', 'Wb2', 'bn_b2', 'Wt2', 'bn_t2', 'Wb3', 'bn_b3', 'bn_p3', 'Wb4', 'bn_b4')}
    del _L0_conv_all

    def _L1_attn_setup():
        import jax, jax.numpy as jnp
        import numpy as np
        EMBED_DIM = 32
        GAMMA = 1.0
        B, S = (4, 1024)
        key = jax.random.key(seed)
        ks = jax.random.split(key, 6)
        return {'inputs': jax.random.normal(ks[0], (B, S, EMBED_DIM), dtype=jnp.float32), 'rotation_params': jax.random.normal(ks[1], (EMBED_DIM * EMBED_DIM,), dtype=jnp.float32), 'entangle_params': jax.random.normal(ks[2], (EMBED_DIM * EMBED_DIM,), dtype=jnp.float32), 'Wq': jax.random.normal(ks[3], (EMBED_DIM, EMBED_DIM), dtype=jnp.float32) / np.sqrt(EMBED_DIM), 'Wk': jax.random.normal(ks[4], (EMBED_DIM, EMBED_DIM), dtype=jnp.float32) / np.sqrt(EMBED_DIM), 'Wv': jax.random.normal(ks[5], (EMBED_DIM, EMBED_DIM), dtype=jnp.float32) / np.sqrt(EMBED_DIM)}
    _L1_attn_all = _L1_attn_setup()
    _L1_attn_in = {k: v for k, v in _L1_attn_all.items() if k in ('rotation_params', 'entangle_params', 'Wq', 'Wk', 'Wv')}
    del _L1_attn_all

    def _L1_ffn_setup():
        import jax, jax.numpy as jnp
        import numpy as np
        BN_EPS = 1e-05
        key = jax.random.key(seed)
        k1, k2, k3 = jax.random.split(key, 3)
        B, T, I, H = (16, 512, 32, 32)
        x = jax.random.normal(k1, (B, T, I), dtype=jnp.float32)
        W = jax.random.normal(k2, (H, I), dtype=jnp.float32) * (1.0 / np.sqrt(I))
        V = jnp.linalg.qr(jax.random.normal(k3, (H, H), dtype=jnp.float32))[0]
        gamma = jnp.ones((H,), dtype=jnp.float32)
        beta = jnp.zeros((H,), dtype=jnp.float32)
        return {'x': x, 'W': W, 'V': V, 'gamma': gamma, 'beta': beta}
    _L1_ffn_all = _L1_ffn_setup()
    _L1_ffn_in = {k: v for k, v in _L1_ffn_all.items() if k in ('W', 'V', 'gamma', 'beta')}
    del _L1_ffn_all
    return {'x': x, 'L0_conv_A_learned': _L0_conv_in['A_learned'], 'L0_conv_A_flat': _L0_conv_in['A_flat'], 'L0_conv_A_intra': _L0_conv_in['A_intra'], 'L0_conv_A_inter': _L0_conv_in['A_inter'], 'L0_conv_Wgc': _L0_conv_in['Wgc'], 'L0_conv_bn_gc': _L0_conv_in['bn_gc'], 'L0_conv_Wb1': _L0_conv_in['Wb1'], 'L0_conv_bn_b1': _L0_conv_in['bn_b1'], 'L0_conv_Wt1': _L0_conv_in['Wt1'], 'L0_conv_bn_t1': _L0_conv_in['bn_t1'], 'L0_conv_Wb2': _L0_conv_in['Wb2'], 'L0_conv_bn_b2': _L0_conv_in['bn_b2'], 'L0_conv_Wt2': _L0_conv_in['Wt2'], 'L0_conv_bn_t2': _L0_conv_in['bn_t2'], 'L0_conv_Wb3': _L0_conv_in['Wb3'], 'L0_conv_bn_b3': _L0_conv_in['bn_b3'], 'L0_conv_bn_p3': _L0_conv_in['bn_p3'], 'L0_conv_Wb4': _L0_conv_in['Wb4'], 'L0_conv_bn_b4': _L0_conv_in['bn_b4'], 'L1_attn_rotation_params': _L1_attn_in['rotation_params'], 'L1_attn_entangle_params': _L1_attn_in['entangle_params'], 'L1_attn_Wq': _L1_attn_in['Wq'], 'L1_attn_Wk': _L1_attn_in['Wk'], 'L1_attn_Wv': _L1_attn_in['Wv'], 'L1_ffn_W': _L1_ffn_in['W'], 'L1_ffn_V': _L1_ffn_in['V'], 'L1_ffn_gamma': _L1_ffn_in['gamma'], 'L1_ffn_beta': _L1_ffn_in['beta']}

def reference(x, L0_conv_A_learned, L0_conv_A_flat, L0_conv_A_intra, L0_conv_A_inter, L0_conv_Wgc, L0_conv_bn_gc, L0_conv_Wb1, L0_conv_bn_b1, L0_conv_Wt1, L0_conv_bn_t1, L0_conv_Wb2, L0_conv_bn_b2, L0_conv_Wt2, L0_conv_bn_t2, L0_conv_Wb3, L0_conv_bn_b3, L0_conv_bn_p3, L0_conv_Wb4, L0_conv_bn_b4, L1_attn_rotation_params, L1_attn_entangle_params, L1_attn_Wq, L1_attn_Wk, L1_attn_Wv, L1_ffn_W, L1_ffn_V, L1_ffn_gamma, L1_ffn_beta):
    import jax
    import jax.numpy as jnp

    def _L0_conv_ref(x, A_learned, A_flat, A_intra, A_inter, Wgc, bn_gc, Wb1, bn_b1, Wt1, bn_t1, Wb2, bn_b2, Wt2, bn_t2, Wb3, bn_b3, bn_p3, Wb4, bn_b4):
        import jax, jax.numpy as jnp
        import numpy as np
        B, CIN, COUT, T, V = (32, 32, 32, 16, 25)
        CB = COUT // 4
        K = 5
        EPS = 1e-05

        def _bn(x, p):
            g, b, m, v = (p[0], p[1], p[2], p[3])
            s = g / jnp.sqrt(v + EPS)
            return x * s[None, :, None, None] + (b - m * s)[None, :, None, None]

        def _c1x1(x, W):
            return jnp.einsum('oc,bctv->botv', W, x)

        def _tconv(x, W, d):
            return jax.lax.conv_general_dilated(x, W[:, :, :, None], window_strides=(1, 1), padding=((2 * d, 2 * d), (0, 0)), rhs_dilation=(d, 1), dimension_numbers=('NCHW', 'OIHW', 'NCHW'))
        res = x
        h = CIN // 2
        x = jnp.concatenate([x[:, :h], jnp.einsum('bctv,vw->bctw', x[:, h:], A_flat)], axis=1)
        x = jnp.concatenate([jnp.einsum('bctv,vw->bctw', x[:, :h], A_intra), jnp.einsum('bctv,vw->bctw', x[:, h:], A_inter)], axis=1)
        Al = jnp.abs(A_learned)
        d = jnp.maximum(Al.sum(axis=1), 1e-06) ** (-0.5)
        An = d[:, None] * Al * d[None, :]
        x_agg = jnp.einsum('bctv,vw->bctw', x, An)
        y = jax.nn.relu(_bn(_c1x1(x + x_agg, Wgc), bn_gc))
        b1 = _bn(_tconv(jax.nn.relu(_bn(_c1x1(y, Wb1), bn_b1)), Wt1, 1), bn_t1)
        b2 = _bn(_tconv(jax.nn.relu(_bn(_c1x1(y, Wb2), bn_b2)), Wt2, 2), bn_t2)
        p = jax.nn.relu(_bn(_c1x1(y, Wb3), bn_b3))
        p = jax.lax.reduce_window(p, -jnp.inf, jax.lax.max, (1, 1, 3, 1), (1, 1, 1, 1), ((0, 0), (0, 0), (1, 1), (0, 0)))
        b3 = _bn(p, bn_p3)
        b4 = _bn(_c1x1(y, Wb4), bn_b4)
        out = jnp.concatenate([b1, b2, b3, b4], axis=1)
        return jax.nn.relu(out + res)

    def _L1_attn_ref(inputs, rotation_params, entangle_params, Wq, Wk, Wv):
        import jax, jax.numpy as jnp
        import numpy as np
        EMBED_DIM = 32
        GAMMA = 1.0
        B, S = (4, 1024)
        D = EMBED_DIM
        rot = rotation_params.reshape(D, -1)
        ent = entangle_params.reshape(D, -1)
        rotated = jnp.einsum('bsd,de->bse', inputs, rot)
        entangled = jnp.einsum('bsd,de->bse', inputs, ent)
        Q = jnp.einsum('bsd,ed->bse', rotated, Wq)
        K = jnp.einsum('bsd,ed->bse', entangled, Wk)
        V = jnp.einsum('bsd,ed->bse', inputs, Wv)
        q2 = jnp.sum(Q * Q, axis=-1)
        k2 = jnp.sum(K * K, axis=-1)
        qk = jnp.einsum('bqd,bkd->bqk', Q, K)
        dist2 = q2[:, :, None] + k2[:, None, :] - 2.0 * qk
        scores = jnp.exp(-GAMMA * dist2)
        attn = jax.nn.softmax(scores, axis=-1)
        return jnp.einsum('bqk,bkd->bqd', attn, V)

    def _L1_ffn_ref(x, W, V, gamma, beta):
        import jax, jax.numpy as jnp
        import numpy as np
        BN_EPS = 1e-05
        B, T, H = (x.shape[0], x.shape[1], W.shape[0])
        Wx = jnp.einsum('bti,hi->bth', x, W)
        flat = Wx.reshape(B * T, H)
        mean = jnp.mean(flat, axis=0)
        var = jnp.var(flat, axis=0)
        Wx = ((flat - mean) * jax.lax.rsqrt(var + BN_EPS) * gamma + beta).reshape(B, T, H)
        Vt = V.T

        def step(yt, wx_t):
            yt = jax.nn.sigmoid(wx_t + yt @ Vt)
            return (yt, yt)
        y0 = jnp.zeros((B, H), dtype=Wx.dtype)
        _, ys = jax.lax.scan(step, y0, jnp.swapaxes(Wx, 0, 1))
        return jnp.swapaxes(ys, 0, 1)

    def _gn(v, G=32, eps=1e-05):
        B_, C_, H_, W_ = v.shape
        g = v.reshape(B_, G, C_ // G, H_, W_)
        m = jnp.mean(g, axis=(2, 3, 4), keepdims=True)
        s = jnp.var(g, axis=(2, 3, 4), keepdims=True)
        return ((g - m) / jnp.sqrt(s + eps)).reshape(v.shape)

    def _ln_c(v, eps=1e-06):
        m = jnp.mean(v, axis=1, keepdims=True)
        s = jnp.var(v, axis=1, keepdims=True)
        return (v - m) / jnp.sqrt(s + eps)

    def _ln_t(v, eps=1e-05):
        m = jnp.mean(v, axis=-1, keepdims=True)
        s = jnp.var(v, axis=-1, keepdims=True)
        return (v - m) / jnp.sqrt(s + eps)

    def _to_tokens(v):
        B_, C_, H_, W_ = v.shape
        return v.reshape(B_, C_, H_ * W_).transpose(0, 2, 1)

    def _from_tokens(t, like):
        B_, C_, H_, W_ = like.shape
        return t.transpose(0, 2, 1).reshape(B_, C_, H_, W_)
    x = _L0_conv_ref(x, L0_conv_A_learned, L0_conv_A_flat, L0_conv_A_intra, L0_conv_A_inter, L0_conv_Wgc, L0_conv_bn_gc, L0_conv_Wb1, L0_conv_bn_b1, L0_conv_Wt1, L0_conv_bn_t1, L0_conv_Wb2, L0_conv_bn_b2, L0_conv_Wt2, L0_conv_bn_t2, L0_conv_Wb3, L0_conv_bn_b3, L0_conv_bn_p3, L0_conv_Wb4, L0_conv_bn_b4)
    t = _to_tokens(x)
    t = t + _L1_attn_ref(_ln_t(t), L1_attn_rotation_params, L1_attn_entangle_params, L1_attn_Wq, L1_attn_Wk, L1_attn_Wv)
    t = t + _L1_ffn_ref(_ln_t(t), L1_ffn_W, L1_ffn_V, L1_ffn_gamma, L1_ffn_beta)
    x = _from_tokens(t, x)
    return x

_drawn_inputs = setup_inputs


def setup_inputs(seed=0):
    import zlib

    import numpy as np

    out = dict(_drawn_inputs(seed))
    spreads = {'L1_ffn_gamma': (1.0, 0.587), 'L1_ffn_beta': (0.0, 0.549)}
    factors = {}
    for name, (base, spread) in spreads.items():
        noise = np.random.default_rng([zlib.crc32(name.encode()), seed]).standard_normal(out[name].shape)
        drawn = base * np.exp(spread * noise) if base else spread * noise
        out[name] = jnp.asarray(drawn.astype(out[name].dtype))
    for name, factor in factors.items():
        out[name] = (out[name] * factor).astype(out[name].dtype)
    return out
```

```python
from contextlib import ExitStack

import numpy as np

import concourse.bass as bass
from concourse import mybir

F32 = mybir.dt.float32
BF16 = mybir.dt.bfloat16
I32 = mybir.dt.int32
ALU = mybir.AluOpType
ACT = mybir.ActivationFunctionType

B, C, T, V = 32, 32, 16, 25
N = T * V
NB = 4
G = B // NB
PAIRS = G // 2
P = NB * C
BR, CB, K = 4, C // 4, 5
TT, MT = 4, 100
SHIFTS = (-4, -2, -1, 0, 1, 2, 4)
PAD = 4 * V
BN_EPS = LN_EPS = 1e-5
L = 16
NC = N // L
W = 10
COLS = G * NC
HALF = COLS // 2
ARENA = 2 * NB * TT * N + N
TWO_ONES = float(np.frombuffer(np.uint32(0x3F803F80).tobytes(), np.float32)[0])
MEET = (2.0 ** -18) ** 2

EARLY, LATE = {}, {}


def _place(table, *entries):
    at = 0
    for name, width in entries:
        table[name] = (at, width)
        at += width
    return at


EARLY_W = _place(EARLY, ("mix", 2 * P), ("ident", P), ("al", MT), ("alT", MT), ("intraT", MT), ("interT", MT),
                 ("flatT", MT), ("bn_g", 3), ("bn_b", 3), ("bn_m", 3), ("bn_v", 3), ("keep", 3), ("pass", 3),
                 ("not_first", 1), ("third", 1), ("gamma", 1), ("beta", 1), ("eps", 1), ("ones", C))
LATE_W = _place(LATE, ("branch", P), ("taps", len(SHIFTS) * P), ("center", P), ("mean", P), ("rotT", P),
                ("wqT", P), ("entT", P), ("wkT", P), ("wvT", P), ("selk", P), ("selq", P), ("wT", P), ("w", P),
                ("vT", P), ("avg4", P))


def build(nc, x, early, late, out):
    with ExitStack() as ctx:
        def sb(name, shape, dt=F32):
            return ctx.enter_context(nc.sbuf_tensor(name, shape, dt))

        def sem(name):
            return ctx.enter_context(nc.semaphore(name))

        ce = sb("ce", [P, EARLY_W])
        cl = sb("cl", [P, LATE_W])

        def e_(name, rows=P):
            o, w = EARLY[name]
            return ce[0:rows, o:o + w]

        def l_(name):
            o, w = LATE[name]
            return cl[:, o:o + w]

        t0 = sb("t0", [P, G, N])
        vst = sb("vst", [MT, G, 4 * P])
        stacks = sb("stacks", [P, 4 * B * N // 2])
        arena = sb("arena", [P, ARENA])
        vb = sb("vb", [MT, 2, 4 * P])
        mlo = sb("mlo", [MT, 2, MT])
        t2 = sb("t2", [MT, MT])
        ia = sb("ia", [MT, MT])
        nrm = [sb(f"nrm{h}", [P, N])[:, :] for h in range(2)]
        dd = sb("dd", [MT, MT])
        aq = sb("aq", [P, 2, P])
        small = sb("small", [P, 64])
        flag = sb("flag", [1, 1], I32)
        ps = ctx.enter_context(nc.psum_tensor("ps", [P, 8, 512], F32))

        def stack(n):
            w = B * N // 2
            return stacks[:, n * w:(n + 1) * w].bitcast(BF16).rearrange("p (b n) -> p b n", n=N)

        ka, kb, qa, qb = (stack(n) for n in range(4))

        cut = [0]

        def piece(width, dt=F32):
            a = arena[:, cut[0]:cut[0] + width]
            cut[0] += width
            return a if dt == F32 else a.bitcast(dt)

        xt = [piece(N) for _ in range(2)]
        z1 = [piece(4 * 2 * P) for _ in range(2)]
        y4 = [piece(N) for _ in range(2)]
        zp = [piece(N + 2 * PAD) for _ in range(2)]
        mx = [piece(N) for _ in range(2)]
        ts = [piece(N) for _ in range(2)]
        sq = [piece(N) for _ in range(2)]
        xl = [piece(N) for _ in range(2)]
        kp = [piece(3 * N // 2, BF16).rearrange("p (s n) -> p s n", n=N) for _ in range(2)]
        qp = [piece(3 * N // 2, BF16).rearrange("p (s n) -> p s n", n=N) for _ in range(2)]
        ep = [piece(3 * N // 2, BF16).rearrange("p (s n) -> p s n", n=N) for _ in range(2)]
        std, rstd, sqk, sqq, rk, rq = ts, y4, sq, ts, mx, y4
        es = [z[:, 0:N] for z in z1]
        er = [z[:, N:2 * N] for z in z1]
        assert cut[0] <= ARENA
        w_half = NB * TT * N
        prob = [arena[0:MT, h * w_half:(h + 1) * w_half].rearrange("p (b k n) -> p b k n", b=NB, k=TT)
                for h in range(2)]
        rden = arena[:, 2 * w_half:2 * w_half + N]
        xl2 = stacks[:, 0:L * COLS].rearrange("p (s g c) -> p s g c", s=L, g=G)
        yb = stacks[:, 3200:3200 + (L + 1) * COLS].rearrange("p (s g c) -> p s g c", s=L + 1, g=G)
        ys = stacks[:, 6600:6600 + COLS].rearrange("p (g c) -> p g c", g=G)
        yd = stacks[:, 6800:6800 + COLS].rearrange("p (g c) -> p g c", g=G)
        sq2 = [stacks[:, 7000 + n * N:7000 + (n + 1) * N] for n in range(2)]
        sd2 = [stacks[:, 7800 + n * N:7800 + (n + 1) * N] for n in range(2)]
        rs2 = [stacks[:, 8600 + n * N:8600 + (n + 1) * N] for n in range(2)]
        xc2 = [stacks[:, 9400 + n * N:9400 + (n + 1) * N] for n in range(2)]
        outs = stacks[:, 10200:10200 + G * N].rearrange("p (g n) -> p g n", n=N)
        stat = sb("stat", [P, G, 6])
        wsc = sb("wsc", [P, P])
        diag = sb("diag", [P, P])

        dk = nc.dram_tensor("dk", [G, 3, P, N], BF16, kind="Internal").ap()
        dq = nc.dram_tensor("dq", [G, 3, P, N], BF16, kind="Internal").ap()
        de = nc.dram_tensor("de", [G, P, N], BF16, kind="Internal").ap()

        def col(n, w=1, rows=P):
            return small[0:rows, n:n + w]

        rowsum, dmax, dsq, dcol = (col(n, 1, MT) for n in range(4))
        bn_sd, bn_r, bn_s, bn_ms, bn_h = (col(4 + 3 * n, 3) for n in range(5))
        bn_s2, bn_h2 = col(19, 3), col(22, 3)
        mv, mm, tot, m2, vv, sdv, rsv, scl, msc, shf = (col(25, 2), col(27, 2), col(29, 2), col(31), col(32),
                                                        col(33), col(34), col(35), col(36), col(37))
        okc, okt = col(38), col(39)
        S_GC, S_Z, S_POST = 0, 1, 2

        (x_in, early_in, late_in, one_rows, scratch_in, stack_in, out_done) = (
            sem(n) for n in ("x_in", "early_in", "late_in", "one_rows", "scratch_in", "stack_in", "out_done"))
        (zeroed, abs_done, dve_c, act_c, pe_c, prep_done) = (
            sem(n) for n in ("zeroed", "abs_done", "dve_c", "act_c", "pe_c", "prep_done"))
        (s1_done, z1_ready, y_done, y_ready, z_done, zb_ready, mx_ready, pooled, t_done, ts_ready, t0_ready,
         c_done, sq_ready, var_done, std_ready, rstd_ready, xl_ready, kqv_done, k1_ready, q1_ready, v_ready,
         rk_ready, rq_ready, k2_ready, parts_ready, e_done, es_ready, e_step, e_ready) = (
            sem(n) for n in ("s1_done", "z1_ready", "y_done", "y_ready", "z_done", "zb_ready", "mx_ready",
                             "pooled", "t_done", "ts_ready", "t0_ready", "c_done", "sq_ready", "var_done",
                             "std_ready", "rstd_ready", "xl_ready", "kqv_done", "k1_ready", "q1_ready",
                             "v_ready", "rk_ready", "rq_ready", "k2_ready", "parts_ready", "e_done",
                             "es_ready", "e_step", "e_ready"))
        (s_done, e1_done, p_ready, vb_ready, pv_done, rden_ready, nrm_ready, t1_ready) = (
            sem(n) for n in ("s_done", "e1_done", "p_ready", "vb_ready", "pv_done", "rden_ready",
                             "nrm_ready", "t1_ready"))
        (c2_done, sq2_ready, var2_done, sd2_ready, rs2_ready, xl2_ready, wx_done, st_ready, bn_c, bn_pe, bn_act,
         wsc_ready) = (
            sem(n) for n in ("c2_done", "sq2_ready", "var2_done", "sd2_ready", "rs2_ready", "xl2_ready",
                             "wx_done", "st_ready", "bn_c", "bn_pe", "bn_act", "wsc_ready"))
        pre = [sem("pre0"), sem("pre1")]
        y_ok = [sem("y_ok0"), sem("y_ok1")]
        (start_ok, cmp_c, cmp_pe, flag_ok, y_final, add_a, add_b) = (
            sem(n) for n in ("start_ok", "cmp_c", "cmp_pe", "flag_ok", "y_final", "add_a", "add_b"))

        block = ctx.enter_context(nc.Block())

        def bank(par, n):
            return 4 * par + n

        def at(t, g):
            return t[:, bass.ds(g, 1), :].rearrange("p o n -> p (o n)")

        def apart(eng):
            eng.wait_ge(early_in, 16)

        @block.sync
        def _(sp):
            sp.dma_start(ce[:, :], early).then_inc(early_in, 16)

            def load(g, par):
                sp.dma_start(xt[par], x[bass.ds(g, 1), :, :].rearrange("o p n -> p (o n)")).then_inc(x_in, 16)

            load(0, 0)
            load(1, 1)
            sp.wait_ge(zeroed, 6)
            sp.dma_start(kb[67:70, :, :], qb[64:67, :, :]).then_inc(one_rows, 16)
            sp.sem_inc(scratch_in, 48)

            def block_in(dst, first, rows, src, g):
                sp.dma_start(dst[first:first + rows, bass.ds(NB * g, NB), :], src).then_inc(stack_in, 16)

            def stack_parts(g, par):
                sp.wait_ge(parts_ready, 2 * g + 2)
                for scratch, parts in ((dk, kp), (dq, qp)):
                    sp.dma_start(scratch[bass.ds(g, 1)].rearrange("o s p n -> p (o s) n"),
                                 parts[par]).then_inc(scratch_in, 16)
                sp.wait_ge(e_ready, g + 2)
                sp.dma_start(de[bass.ds(g, 1)].rearrange("o p n -> p (o n)"), ep[par][:, 2, :]).then_inc(scratch_in, 16)
                sp.wait_ge(scratch_in, 48 * g + 96)
                for dst, scratch, parts in ((ka, dk, (0, 0, 1, 1)), (qa, dq, (0, 1, 0, 1)),
                                            (kb, dk, (0, 2)), (qb, dq, (2, 0))):
                    for j, s in enumerate(parts):
                        block_in(dst, C * j, C, scratch[bass.ds(g, 1), s].rearrange("o (b c) n -> c (o b) n", b=NB), g)
                rows = de[bass.ds(g, 1)].rearrange("o (b r) n -> r (o b) n", b=NB)
                block_in(kb, 2 * C, 3, rows[0:3], g)
                block_in(qb, 2 * C + 3, 3, rows[3:6], g)

            with sp.Fori(0, PAIRS - 1) as i:
                for par in range(2):
                    sp.wait_ge(ts_ready, 2 * i + par + 1)
                    load(2 * i + 2 + par, par)
                for par in range(2):
                    stack_parts(2 * i + par, par)
            for par in range(2):
                stack_parts(G - 2 + par, par)
            with sp.Fori(0, PAIRS) as i:
                for par, added in ((0, add_a), (1, add_b)):
                    g = 2 * i + par
                    sp.wait_ge(added, i + 1)
                    sp.dma_start(out[bass.ds(g, 1)].rearrange("o p n -> p (o n)"), at(outs, g)).then_inc(out_done, 16)
            sp.wait_ge(out_done, 16 * G)

        @block.gpsimd
        def _(pool):
            fills = [(zp[h][:, o:o + PAD], 0.0) for h in range(2) for o in (0, PAD + N)]
            fills += [(t[64:96, :, :].rearrange("p b n -> p (b n)").bitcast(F32), v) for t, v in ((kb, 0.0), (qb, TWO_ONES))]
            for n, (t, v) in enumerate(fills):
                if n:
                    pool.wait_ge(zeroed, n)
                nc.gpsimd.memset(t, v).then_inc(zeroed, 1)
            pool.wait_ge(zeroed, len(fills))
            pool.wait_ge(early_in, 16)
            with pool.Fori(0, PAIRS) as i:
                for par in range(2):
                    g = 2 * i + par
                    a, b, f = (ep[par][:, s, :] for s in range(3))
                    pool.wait_ge(es_ready, g + 1)
                    pool.wait_ge(scratch_in, 48 * g)
                    nc.gpsimd.tensor_tensor(a, es[par], e_("not_first").to_broadcast([P, N]), ALU.mult).then_inc(e_step, 1)
                    pool.wait_ge(e_step, 3 * g + 1)
                    nc.gpsimd.tensor_tensor(er[par], es[par], a, ALU.add).then_inc(e_step, 1)
                    pool.wait_ge(e_step, 3 * g + 2)
                    nc.gpsimd.tensor_tensor(b, er[par], e_("third").to_broadcast([P, N]), ALU.mult).then_inc(e_step, 1)
                    pool.wait_ge(e_step, 3 * g + 3)
                    nc.gpsimd.tensor_tensor(f, er[par], b, ALU.add).then_inc(e_ready, 1)
            def values(g, par):
                pool.wait_ge(v_ready, g + 1)
                pool.wait_ge(pv_done, g)
                apart(pool)
                nc.gpsimd.tensor_copy(vb[:, par, :], at(vst, g)).then_inc(vb_ready, 1)

            def residual(g, par):
                pool.wait_ge(nrm_ready, g + 2)
                nc.gpsimd.tensor_tensor(at(t0, g), at(t0, g), nrm[par], ALU.add).then_inc(t1_ready, 1)

            for par in range(2):
                values(par, par)
            with pool.Fori(0, PAIRS - 1) as i:
                for par in range(2):
                    residual(2 * i + par, par)
                    values(2 * i + 2 + par, par)
            for par in range(2):
                residual(G - 2 + par, par)
            pool.wait_ge(y_final, 1)
            with pool.Fori(0, PAIRS) as i:
                g = 2 * i + 1
                nc.gpsimd.tensor_tensor(
                    at(outs, g).rearrange("p (c s) -> p c s", s=L), at(t0, g).rearrange("p (c s) -> p c s", s=L),
                    yb[:, 1:L + 1, bass.ds(g, 1), :].rearrange("p s o c -> p c (o s)"), ALU.add).then_inc(add_b, 1)

        @block.scalar
        def _(act):
            act.dma_start(cl[:, :], late).then_inc(late_in, 16)
            act.wait_ge(early_in, 16)
            nc.scalar.activation(dd[:, :], e_("al", MT), ACT.Abs, accum_out=rowsum)
            nc.scalar.activation(t2[:, :], e_("alT", MT), ACT.Abs).then_inc(abs_done, 1)
            nc.scalar.activation(bn_sd, e_("bn_v"), ACT.Sqrt, bias=e_("eps")).then_inc(act_c, 1)
            act.wait_ge(dve_c, 1)
            nc.scalar.activation(dsq, dmax, ACT.Sqrt).then_inc(act_c, 1)
            act.wait_ge(prep_done, 1)
            act.sem_inc(p_ready, 1)
            with act.Fori(0, PAIRS) as i:
                for par in range(2):
                    g = 2 * i + par
                    act.wait_ge(y_done, g + 1)
                    nc.scalar.activation(y4[par], ps[:, bank(par, 2), 0:N], ACT.Relu, bias=bn_h2[:, S_GC:S_GC + 1],
                                         scale=bn_s2[:, S_GC:S_GC + 1]).then_inc(y_ready, 1)
                for par in range(2):
                    g = 2 * i + par
                    act.wait_ge(z_done, g + 1)
                    for lo, hi, f in ((0, 96, ACT.Relu), (96, P, ACT.Identity)):
                        last = nc.scalar.activation(zp[par][lo:hi, PAD:PAD + N], ps[lo:hi, bank(par, 3), 0:N], f,
                                                    bias=bn_h2[lo:hi, S_Z:S_Z + 1], scale=bn_s2[lo:hi, S_Z:S_Z + 1])
                    last.then_inc(zb_ready, 1)
                for par in range(2):
                    g = 2 * i + par
                    act.wait_ge(ts_ready, g + 1)
                    nc.scalar.activation(at(t0, g), ts[par], ACT.Relu,
                                         bias=bn_h2[:, S_POST:S_POST + 1]).then_inc(t0_ready, 1)
                for par in range(2):
                    g = 2 * i + par
                    act.wait_ge(c_done, g + 1)
                    nc.scalar.activation(sq[par], ps[:, bank(par, 1), 0:N], ACT.Square).then_inc(sq_ready, 1)
                for par in range(2):
                    g = 2 * i + par
                    act.wait_ge(var_done, g + 1)
                    nc.scalar.activation(std[par], ps[:, bank(par, 2), 0:N], ACT.Sqrt,
                                         bias=e_("eps")).then_inc(std_ready, 1)
                for par in range(2):
                    g = 2 * i + par
                    act.wait_ge(kqv_done, g + 1)
                    act.wait_ge(scratch_in, 48 * g)
                    for parts, s, n, ready in ((kp, sqk, 3, k1_ready), (qp, sqq, 0, q1_ready)):
                        nc.scalar.copy(parts[par][:, 0, :], ps[:, bank(par, n), 0:N])
                        nc.scalar.activation(s[par], ps[:, bank(par, n), 0:N], ACT.Square).then_inc(ready, 1)
                    nc.scalar.copy(at(vst, g), ps[0:MT, bank(par, 1), :]).then_inc(v_ready, 1)
                for par in range(2):
                    g = 2 * i + par
                    act.wait_ge(e_done, g + 1)
                    nc.scalar.copy(es[par], ps[:, bank(par, 2), 0:N]).then_inc(es_ready, 1)

            def unit(g, par, u):
                n, slot = 8 * g + u, u % 2
                act.wait_ge(s_done, n + 1)
                s = ps[0:MT, 2 * slot:2 * slot + 2, 0:N]
                nc.scalar.activation(s, s, ACT.Exp, scale=2.0).then_inc(e1_done, 1)
                act.wait_ge(e1_done, n + 1)
                k = 2 * (u % 2)
                nc.scalar.activation(prob[par][:, u // 2, k:k + 2, :], s, ACT.Exp).then_inc(p_ready, 1)

            act.wait_ge(scratch_in, 48 * (G + 1))
            with act.Fori(0, PAIRS) as i:
                for par in range(2):
                    g = 2 * i + par
                    act.wait_ge(pv_done, g)
                    for u in range(8):
                        unit(g, par, u)

            with act.Fori(0, PAIRS) as i:
                for par in range(2):
                    act.wait_ge(c2_done, 2 * i + par + 1)
                    nc.scalar.activation(sq2[par], ps[:, bank(par, 0), 0:N], ACT.Square).then_inc(sq2_ready, 1)
                for par in range(2):
                    act.wait_ge(var2_done, 2 * i + par + 1)
                    nc.scalar.activation(sd2[par], ps[:, bank(par, 1), 0:N], ACT.Sqrt,
                                         bias=e_("eps")).then_inc(sd2_ready, 1)
            act.wait_ge(bn_c, 4)
            nc.scalar.activation(sdv, vv, ACT.Sqrt, bias=e_("eps")).then_inc(bn_act, 1)
            act.wait_ge(wsc_ready, 1)
            act.wait_ge(bn_c, 9)

            def steps(base, count):
                with act.Fori(0, count // 2) as i:
                    for par in range(2):
                        s = 2 * i + par
                        for h in range(2):
                            act.wait_ge(pre[h], base + s + 1)
                            nc.scalar.activation(
                                yb[:, bass.ds(s + 1, 1), 4 * h:4 * h + 4, :].rearrange("p o g c -> p (o g c)"),
                                ps[:, 2 * h + par, 0:HALF], ACT.Sigmoid, bias=shf).then_inc(y_ok[h], 1)

            steps(0, L)
            steps(L, W)
            act.wait_ge(flag_ok, 1)
            with act.If(act.value_load(flag[0:1, 0:1], min_val=0, max_val=1) != 0):
                with act.Fori(0, NC - 1) as k:
                    steps(L + W + L * k, L)

        @block.vector
        def _(dve):
            count = [0]

            def link(ins, s=dve_c, c=count):
                c[0] += 1
                ins.then_inc(s, 1)
                dve.wait_ge(s, c[0])

            dve.wait_ge(early_in, 16)
            dve.wait_ge(abs_done, 1)
            link(nc.vector.tensor_scalar(dmax, rowsum, 1e-6, None, ALU.max))
            dve.wait_ge(act_c, 2)
            link(nc.vector.reciprocal(dcol, dsq))
            link(nc.vector.tensor_scalar(dd[:, :], e_("ident", MT)[:, 0:MT], dcol, None, ALU.mult))
            link(nc.vector.reciprocal(bn_r, bn_sd))
            link(nc.vector.tensor_tensor(bn_s, bn_r, e_("bn_g"), ALU.mult))
            link(nc.vector.tensor_tensor(bn_ms, bn_s, e_("bn_m"), ALU.mult))
            link(nc.vector.tensor_tensor(bn_h, e_("bn_b"), bn_ms, ALU.subtract))
            link(nc.vector.tensor_tensor(bn_h2, bn_h, e_("keep"), ALU.mult))
            link(nc.vector.tensor_tensor(bn_s, bn_s, e_("keep"), ALU.mult))
            link(nc.vector.tensor_tensor(bn_s2, bn_s, e_("pass"), ALU.add))
            dve.wait_ge(pe_c, 3)
            link(nc.vector.scalar_tensor_tensor(out=ia[:, :], in0=ps[0:MT, 2, 0:MT], scalar=dcol,
                                                in1=e_("ident", MT)[:, 0:MT], op0=ALU.mult, op1=ALU.add))
            nc.vector.tensor_copy(aq[:, 0, :], ps[:, 6, 0:P])
            link(nc.vector.tensor_copy(aq[:, 1, :], ps[:, 7, 0:P]))
            dve.wait_ge(pe_c, 5)
            nc.vector.tensor_copy(mlo[:, 0, :], ps[0:MT, 2, 0:MT])
            link(nc.vector.tensor_copy(t2[:, :], ps[0:MT, 3, 0:MT]))
            dve.wait_ge(pe_c, 6)
            nc.vector.tensor_copy(mlo[:, 1, :], ps[0:MT, 6, 0:MT]).then_inc(prep_done, 1)
            dve.wait_ge(zeroed, 4)

            with dve.Fori(0, PAIRS) as i:
                for par in range(2):
                    g = 2 * i + par
                    dve.wait_ge(s1_done, g + 1)
                    dve.wait_ge(e_ready, g)
                    nc.vector.tensor_copy(z1[par][0:MT, :].rearrange("p (k n) -> p k n", k=2),
                                          ps[0:MT, bank(par, 0):bank(par, 2), :]).then_inc(z1_ready, 1)
                for par in range(2):
                    g = 2 * i + par
                    mid = zp[par][64:96, PAD:PAD + N]
                    dve.wait_ge(zb_ready, g + 1)
                    nc.vector.tensor_tensor(mx[par][64:96, :], zp[par][64:96, PAD - V:PAD - V + N],
                                            zp[par][64:96, PAD + V:PAD + V + N], ALU.max).then_inc(mx_ready, 1)
                    dve.wait_ge(mx_ready, g + 1)
                    nc.vector.tensor_tensor(mid, mid, mx[par][64:96, :], ALU.max).then_inc(pooled, 1)
                for par in range(2):
                    g = 2 * i + par
                    dve.wait_ge(t_done, g + 1)
                    nc.vector.scalar_tensor_tensor(out=ts[par], in0=ps[:, bank(par, 0), 0:N],
                                                   scalar=bn_s2[:, S_POST:S_POST + 1], in1=xt[par],
                                                   op0=ALU.mult, op1=ALU.add).then_inc(ts_ready, 1)
                for par in range(2):
                    g = 2 * i + par
                    dve.wait_ge(std_ready, g + 1)
                    nc.vector.reciprocal(rstd[par], std[par]).then_inc(rstd_ready, 1)
                    dve.wait_ge(rstd_ready, g + 1)
                    nc.vector.tensor_tensor(xl[par], ps[:, bank(par, 1), 0:N], rstd[par],
                                            ALU.mult).then_inc(xl_ready, 1)
                for par in range(2):
                    g = 2 * i + par
                    dve.wait_ge(k1_ready, g + 1)
                    nc.vector.tensor_tensor(rk[par], ps[:, bank(par, 3), 0:N], kp[par][:, 0, :],
                                            ALU.subtract).then_inc(rk_ready, 1)
                    dve.wait_ge(q1_ready, g + 1)
                    nc.vector.tensor_tensor(rq[par], ps[:, bank(par, 0), 0:N], qp[par][:, 0, :],
                                            ALU.subtract).then_inc(rq_ready, 1)
                for par in range(2):
                    g = 2 * i + par
                    for n, (r, parts) in enumerate(((rk, kp), (rq, qp))):
                        dve.wait_ge((rk_ready, rq_ready)[n], g + 1)
                        nc.vector.tensor_copy(parts[par][:, 1, :], r[par]).then_inc(k2_ready, 1)
                    for n, (r, parts) in enumerate(((rk, kp), (rq, qp))):
                        dve.wait_ge(k2_ready, 2 * g + n + 1)
                        nc.vector.tensor_tensor(parts[par][:, 2, :], r[par], parts[par][:, 1, :],
                                                ALU.subtract).then_inc(parts_ready, 1)

            with dve.Fori(0, PAIRS) as i:
                for par in range(2):
                    g = 2 * i + par
                    dve.wait_ge(pv_done, g + 2)
                    dve.wait_ge(nrm_ready, g + 1)
                    nc.vector.reciprocal(rden, ps[:, 5 + 2 * par, 0:N]).then_inc(rden_ready, 1)
                    dve.wait_ge(rden_ready, g + 1)
                    dve.wait_ge(t1_ready, g)
                    nc.vector.tensor_tensor(nrm[par], ps[:, 4 + 2 * par, 0:N], rden,
                                            ALU.mult).then_inc(nrm_ready, 1)

            with dve.Fori(0, PAIRS) as i:
                for par in range(2):
                    g = 2 * i + par
                    dve.wait_ge(sd2_ready, g + 1)
                    nc.vector.reciprocal(rs2[par], sd2[par]).then_inc(rs2_ready, 1)
                    dve.wait_ge(rs2_ready, g + 1)
                    nc.vector.tensor_tensor(xc2[par], ps[:, bank(par, 0), 0:N], rs2[par],
                                            ALU.mult).then_inc(xl2_ready, 1)
                for par in range(2):
                    g = 2 * i + par
                    dve.wait_ge(xl2_ready, 2 * i + 2)
                    nc.vector.tensor_copy(xl2[:, :, bass.ds(g, 1), :].rearrange("p s o c -> p c (o s)"),
                                          xc2[par].rearrange("p (c s) -> p c s", s=L)).then_inc(st_ready, 1)
                    dve.wait_ge(wx_done, g + 1)
                    nc.vector.bn_stats(at(stat, g), ps[:, bank(par, 2), 0:N]).then_inc(st_ready, 1)
            bc = [0]

            def blink(ins):
                link(ins, bn_c, bc)

            dve.wait_ge(st_ready, 2 * G)
            blink(nc.vector.bn_aggr(mv, stat[:, :, :].rearrange("p g s -> p (g s)")))
            blink(nc.vector.tensor_tensor(m2, mv[:, 0:1], mv[:, 0:1], ALU.mult))
            nc.vector.tensor_copy(mm[:, 0:1], mv[:, 0:1])
            blink(nc.vector.tensor_tensor(mm[:, 1:2], mv[:, 1:2], m2, ALU.add))
            dve.wait_ge(bn_pe, 1)
            nc.vector.tensor_copy(tot, ps[:, 3, 0:2]).then_inc(cmp_c, 1)
            dve.wait_ge(cmp_c, 1)
            nc.vector.tensor_tensor(m2, tot[:, 0:1], tot[:, 0:1], ALU.mult).then_inc(cmp_c, 1)
            dve.wait_ge(cmp_c, 2)
            blink(nc.vector.tensor_tensor(vv, tot[:, 1:2], m2, ALU.subtract))
            dve.wait_ge(bn_act, 1)
            blink(nc.vector.reciprocal(rsv, sdv))
            blink(nc.vector.tensor_tensor(scl, rsv, e_("gamma"), ALU.mult))
            blink(nc.vector.tensor_scalar(diag[:, :], e_("ident"), scl, None, ALU.mult))
            blink(nc.vector.tensor_tensor(msc, tot[:, 0:1], scl, ALU.mult))
            blink(nc.vector.tensor_tensor(shf, e_("beta"), msc, ALU.subtract))
            nc.vector.memset(yb[:, 0, :, :], 0.0).then_inc(start_ok, 1)
            dve.wait_ge(bn_pe, 2)
            nc.vector.tensor_copy(wsc[:, :], ps[:, 7, 0:P]).then_inc(wsc_ready, 1)

            def chain(base):
                for h in range(2):
                    dve.wait_ge(y_ok[h], base + 1)
                nc.vector.tensor_copy(yb[:, 0, :, 1:NC], yb[:, L, :, 0:NC - 1]).then_inc(start_ok, 1)

            for h in range(2):
                dve.wait_ge(y_ok[h], L + 1)
            nc.vector.tensor_copy(ys, yb[:, W, :, :]).then_inc(cmp_c, 1)
            chain(L)
            for h in range(2):
                dve.wait_ge(y_ok[h], L + W + 1)
            dve.wait_ge(cmp_c, 3)
            nc.vector.tensor_tensor(yd, yb[:, W, :, :], ys, ALU.subtract).then_inc(cmp_c, 1)
            dve.wait_ge(cmp_c, 4)
            nc.vector.tensor_tensor(ys, yd, yd, ALU.mult).then_inc(cmp_c, 1)
            dve.wait_ge(cmp_c, 5)
            nc.vector.tensor_scalar(yd, ys, MEET, None, ALU.is_le, ALU.add, accum_out=okc).then_inc(cmp_c, 1)
            dve.wait_ge(cmp_pe, 1)
            nc.vector.tensor_scalar(flag[0:1, 0:1], ps[0:1, 7, 0:1], float(P * COLS), None,
                                    ALU.not_equal).then_inc(flag_ok, 1)
            dve.wait_ge(flag_ok, 1)
            with dve.If(dve.value_load(flag[0:1, 0:1], min_val=0, max_val=1) != 0):
                with dve.Fori(0, NC - 1) as k:
                    chain(L + W + L * k)
                for h in range(2):
                    dve.wait_ge(y_ok[h], L + W + L * (NC - 1) + 1)
            dve.sem_inc(y_final, 1)
            with dve.Fori(0, PAIRS) as i:
                g = 2 * i
                nc.vector.tensor_tensor(
                    at(outs, g).rearrange("p (c s) -> p c s", s=L), at(t0, g).rearrange("p (c s) -> p c s", s=L),
                    yb[:, 1:L + 1, bass.ds(g, 1), :].rearrange("p s o c -> p c (o s)"), ALU.add).then_inc(add_a, 1)

        @block.tensor
        def _(pe):
            mm_ = nc.tensor.matmul
            pe.sem_inc(pv_done, 1)
            for h in range(2):
                pe.sem_inc(y_ok[h], 1)
            pe.sem_inc(e_ready, 1)
            pe.sem_inc(t1_ready, 1)
            pe.sem_inc(nrm_ready, 1)
            pe.wait_ge(late_in, 16)
            mm_(ps[:, 6, 0:P], l_("rotT"), l_("wqT"), start=True, stop=True).then_inc(pe_c, 1)
            mm_(ps[:, 7, 0:P], l_("entT"), l_("wkT"), start=True, stop=True).then_inc(pe_c, 1)
            pe.wait_ge(dve_c, 3)
            mm_(ps[0:MT, 2, 0:MT], t2[:, :], dd[:, :], start=True, stop=True).then_inc(pe_c, 1)
            pe.wait_ge(dve_c, 12)
            mm_(ps[0:MT, 2, 0:MT], e_("intraT", MT), ia[:, :], start=True, stop=True).then_inc(pe_c, 1)
            mm_(ps[0:MT, 3, 0:MT], e_("interT", MT), ia[:, :], start=True, stop=True).then_inc(pe_c, 1)
            pe.wait_ge(dve_c, 13)
            mm_(ps[0:MT, 6, 0:MT], e_("flatT", MT), t2[:, :], start=True, stop=True).then_inc(pe_c, 1)
            pe.wait_ge(prep_done, 1)

            with pe.Fori(0, PAIRS) as i:
                pe.wait_ge(x_in, 32 * i + 32)
                for par in range(2):
                    g = 2 * i + par
                    pe.wait_ge(v_ready, 2 * i)
                    pe.wait_ge(rq_ready, 2 * i)
                    for tt in range(TT):
                        last = mm_(ps[0:MT, bank(par, tt // 2), 256 * (tt % 2):256 * (tt % 2) + 256],
                                   xt[par][:, MT * tt:MT * tt + MT], e_("mix"), start=True, stop=True,
                                   skip_group_check=True)
                    last.then_inc(s1_done, 1)
                for par in range(2):
                    g = 2 * i + par
                    pe.wait_ge(z1_ready, g + 1)
                    pe.wait_ge(es_ready, 2 * i)
                    for tt in range(TT):
                        for h in range(2):
                            last = mm_(ps[:, bank(par, 2), MT * tt:MT * tt + MT],
                                       z1[par][0:MT, 256 * tt + P * h:256 * tt + P * h + P], mlo[:, h, :],
                                       start=(h == 0), stop=(h == 1))
                    last.then_inc(y_done, 1)
                for par in range(2):
                    g = 2 * i + par
                    pe.wait_ge(y_ready, g + 1)
                    pe.wait_ge(rk_ready, 2 * i)
                    mm_(ps[:, bank(par, 3), 0:N], l_("branch"), y4[par], start=True, stop=True).then_inc(z_done, 1)
                for par in range(2):
                    g = 2 * i + par
                    pe.wait_ge(pooled, g + 1)
                    for n, d in enumerate(SHIFTS):
                        o = LATE["taps"][0] + n * P
                        last = mm_(ps[:, bank(par, 0), 0:N], cl[:, o:o + P], zp[par][:, PAD + V * d:PAD + V * d + N],
                                   start=(n == 0), stop=(n == len(SHIFTS) - 1))
                    last.then_inc(t_done, 1)
                for par in range(2):
                    g = 2 * i + par
                    pe.wait_ge(t0_ready, g + 1)
                    mm_(ps[:, bank(par, 1), 0:N], l_("center"), at(t0, g), start=True, stop=True).then_inc(c_done, 1)
                for par in range(2):
                    g = 2 * i + par
                    pe.wait_ge(sq_ready, g + 1)
                    mm_(ps[:, bank(par, 2), 0:N], l_("mean"), sq[par], start=True, stop=True).then_inc(var_done, 1)
                for par in range(2):
                    g = 2 * i + par
                    pe.wait_ge(xl_ready, g + 1)
                    mm_(ps[:, bank(par, 3), 0:N], aq[:, 1, :], xl[par], start=True, stop=True)
                    mm_(ps[:, bank(par, 0), 0:N], aq[:, 0, :], xl[par], start=True, stop=True)
                    for tt in range(TT):
                        last = mm_(ps[0:MT, bank(par, 1), P * tt:P * tt + P], xl[par][:, MT * tt:MT * tt + MT],
                                   l_("wvT"), start=True, stop=True, skip_group_check=True)
                    last.then_inc(kqv_done, 1)
                for par in range(2):
                    g = 2 * i + par
                    pe.wait_ge(k1_ready, g + 1)
                    mm_(ps[:, bank(par, 2), 0:N], l_("selk"), sqk[par], start=True, stop=False)
                    pe.wait_ge(q1_ready, g + 1)
                    mm_(ps[:, bank(par, 2), 0:N], l_("selq"), sqq[par], start=False, stop=True).then_inc(e_done, 1)

            pe.wait_ge(stack_in, 16 * 14 * G)
            pe.wait_ge(one_rows, 16)
            pe.wait_ge(es_ready, G)
            pe.wait_ge(v_ready, G)
            pe.wait_ge(rq_ready, G)

            def scores(g, u):
                n, slot, b = 8 * g + u, u % 2, u // 2
                pe.wait_ge(p_ready, n)
                for k in range(2):
                    o = MT * (2 * (u % 2) + k)
                    dst = ps[0:MT, 2 * slot + k, 0:N]
                    for kk, qq, rows, first in ((ka, qa, P, True), (kb, qb, 96, False)):
                        last = mm_(dst, kk[0:rows, bass.ds(NB * g + b, 1), o:o + MT].rearrange("p o n -> p (o n)"),
                                   qq[0:rows, bass.ds(NB * g + b, 1), :].rearrange("p o n -> p (o n)"),
                                   start=first, stop=not first)
                last.then_inc(s_done, 1)

            def products(par, u):
                k, sums = u // 2, u % 2
                for b in range(NB):
                    w = e_("ones", MT) if sums else vb[:, par, P * k + C * b:P * k + C * b + C]
                    last = mm_(ps[C * b:C * b + C, 4 + 2 * par + sums, 0:N], w, prob[par][:, b, k, :],
                               start=(k == 0), stop=(k == TT - 1), skip_group_check=True)
                return last

            def ready(g):
                pe.wait_ge(p_ready, 8 * g + 9)
                pe.wait_ge(vb_ready, g + 1)
                pe.wait_ge(nrm_ready, g)

            def group(g, prev, par):
                scores(g, 0)
                for u in range(1, 8):
                    scores(g, u)
                    if u == 1:
                        ready(prev)
                    products(par, u - 1)
                products(par, 7).then_inc(pv_done, 1)

            for u in range(8):
                scores(0, u)
            with pe.Fori(0, PAIRS - 1) as i:
                group(2 * i + 1, 2 * i, 0)
                group(2 * i + 2, 2 * i + 1, 1)
            group(G - 1, G - 2, 0)
            ready(G - 1)
            for u in range(8):
                last = products(1, u)
            last.then_inc(pv_done, 1)

            with pe.Fori(0, PAIRS) as i:
                for par in range(2):
                    g = 2 * i + par
                    pe.wait_ge(t1_ready, G + 1)
                    pe.wait_ge(xl2_ready, 2 * i)
                    mm_(ps[:, bank(par, 0), 0:N], l_("center"), at(t0, g), start=True, stop=True).then_inc(c2_done, 1)
                for par in range(2):
                    g = 2 * i + par
                    pe.wait_ge(sq2_ready, g + 1)
                    mm_(ps[:, bank(par, 1), 0:N], l_("mean"), sq2[par], start=True, stop=True).then_inc(var2_done, 1)
                for par in range(2):
                    g = 2 * i + par
                    pe.wait_ge(xl2_ready, g + 1)
                    pe.wait_ge(st_ready, 4 * i)
                    mm_(ps[:, bank(par, 2), 0:N], l_("wT"), xc2[par], start=True, stop=True).then_inc(wx_done, 1)
            pe.wait_ge(bn_c, 3)
            mm_(ps[:, 3, 0:2], l_("avg4"), mm, start=True, stop=True).then_inc(bn_pe, 1)
            pe.wait_ge(bn_c, 7)
            mm_(ps[:, 7, 0:P], l_("w"), diag[:, :], start=True, stop=True).then_inc(bn_pe, 1)
            pe.wait_ge(wsc_ready, 1)

            def steps(base, sweep, count):
                with pe.Fori(0, count // 2) as i:
                    for par in range(2):
                        s = 2 * i + par
                        if par == 0:
                            pe.wait_ge(start_ok, sweep + 1)
                        for h in range(2):
                            pe.wait_ge(y_ok[h], base + s)
                            mm_(ps[:, 2 * h + par, 0:HALF], wsc[:, :],
                                xl2[:, bass.ds(s, 1), 4 * h:4 * h + 4, :].rearrange("p o g c -> p (o g c)"),
                                start=True, stop=False)
                        for h in range(2):
                            pe.wait_ge(y_ok[h], base + s + 1)
                            mm_(ps[:, 2 * h + par, 0:HALF], l_("vT"),
                                yb[:, bass.ds(s, 1), 4 * h:4 * h + 4, :].rearrange("p o g c -> p (o g c)"),
                                start=False, stop=True).then_inc(pre[h], 1)

            steps(0, 0, L)
            steps(L, 1, W)
            pe.wait_ge(cmp_c, 6)
            mm_(ps[0:1, 7, 0:1], okc, e_("ones")[:, 0:1], start=True, stop=True).then_inc(cmp_pe, 1)
            pe.wait_ge(flag_ok, 1)
            with pe.If(pe.value_load(flag[0:1, 0:1], min_val=0, max_val=1) != 0):
                with pe.Fori(0, NC - 1) as k:
                    steps(L + W + L * k, k + 2, L)



def _blocks(a, n):
    r, c = a.shape
    m = np.zeros((n * r, n * c), a.dtype)
    for k in range(n):
        m[k * r:k * r + r, k * c:k * c + c] = a
    return m


def _early(i):
    f = np.float32
    m = np.zeros((P, EARLY_W), f)

    def put(name, a):
        o, w = EARLY[name]
        a = np.asarray(a)
        assert a.shape[1] == w, name
        m[0:a.shape[0], o:o + w] = a

    wgc = i["L0_conv_Wgc"]
    mix = np.zeros((P, 2, P), f)
    h = C // 2
    for b in range(NB):
        for half in range(2):
            mix[C * b + h * half:C * b + h * half + h, half, C * b:C * b + C] = wgc.T[h * half:h * half + h]
    put("mix", mix.reshape(P, 2 * P))
    put("ident", np.eye(P, dtype=f))
    for name, a in (("al", i["L0_conv_A_learned"]), ("alT", i["L0_conv_A_learned"].T), ("intraT", i["L0_conv_A_intra"].T),
                    ("interT", i["L0_conv_A_inter"].T), ("flatT", i["L0_conv_A_flat"].T)):
        put(name, _blocks(a, TT))
    bn = np.ones((4, P, 3), f)
    bn[:, :, 0] = np.tile(i["L0_conv_bn_gc"], (1, NB))
    for j, name in enumerate(("bn_b1", "bn_b2", "bn_b3", "bn_b4")):
        bn[:, C * j:C * j + C, 1] = np.tile(i["L0_conv_" + name], (1, NB))
    for b in range(NB):
        for j, name in enumerate(("bn_t1", "bn_t2", "bn_p3")):
            bn[:, C * b + CB * j:C * b + CB * j + CB, 2] = i["L0_conv_" + name]
    for k, name in enumerate(("bn_g", "bn_b", "bn_m", "bn_v")):
        put(name, bn[k])
    keep = np.ones((P, 3), f)
    keep[np.arange(P) % C >= 3 * CB, 2] = 0
    put("keep", keep)
    put("pass", 1 - keep)
    r = np.arange(P)[:, None] % C
    put("not_first", np.where(np.isin(r, (1, 2, 4, 5)), -1, 0).astype(f))
    put("third", np.where(np.isin(r, (2, 5)), -1, 0).astype(f))
    put("gamma", np.tile(i["L1_ffn_gamma"], NB)[:, None])
    put("beta", np.tile(i["L1_ffn_beta"], NB)[:, None])
    put("eps", np.full((P, 1), LN_EPS, f))
    put("ones", np.ones((P, C), f))
    return m


def _late(i):
    f = np.float32
    m = np.zeros((P, LATE_W), f)

    def put(name, a):
        o, w = LATE[name]
        assert a.shape == (P, w), name
        m[:, o:o + w] = a

    branch = np.zeros((P, BR, NB, CB), f)
    taps = np.zeros((BR, NB, CB, len(SHIFTS), NB, BR, CB), f)
    for b in range(NB):
        for j in range(BR):
            branch[C * b:C * b + C, j, b] = i[f"L0_conv_Wb{j + 1}"].T
        for j, name in enumerate(("Wt1", "Wt2")):
            for k in range(K):
                taps[j, b, :, SHIFTS.index((k - K // 2) * (j + 1)), b, j] = i["L0_conv_" + name][:, :, k].T
        for j in (2, 3):
            taps[j, b, :, SHIFTS.index(0), b, j] = np.eye(CB, dtype=f)
    put("branch", branch.reshape(P, P))
    put("taps", taps.reshape(P, len(SHIFTS) * P))
    mean = np.full((C, C), 1 / C, f)
    put("mean", _blocks(mean, NB))
    put("center", _blocks(np.eye(C, dtype=f) - mean, NB))
    put("rotT", _blocks(i["L1_attn_rotation_params"].reshape(C, C).T, NB))
    put("entT", _blocks(i["L1_attn_entangle_params"].reshape(C, C).T, NB))
    put("wqT", _blocks(i["L1_attn_Wq"].T, NB))
    put("wkT", _blocks(i["L1_attn_Wk"].T, NB))
    put("wvT", _blocks(i["L1_attn_Wv"].T, NB))
    for name, lo in (("selk", 0), ("selq", 3)):
        sel = np.zeros((C, C), f)
        sel[:, lo:lo + 3] = -0.5
        put(name, _blocks(sel, NB))
    put("wT", _blocks(i["L1_ffn_W"].T, NB))
    put("w", _blocks(i["L1_ffn_W"], NB))
    put("vT", _blocks(i["L1_ffn_V"].T, NB))
    put("avg4", np.tile(np.eye(C, dtype=f) / NB, (NB, NB)))
    return m


def kernel(**inputs):
    import concourse.bacc as bacc
    from concourse.bass_utils import run_bass_kernel_spmd

    i = {k: np.asarray(v) for k, v in inputs.items()}
    arrays = {"x": np.ascontiguousarray(i["x"].reshape(G, P, N)), "early": _early(i), "late": _late(i)}
    nc = bacc.Bacc("TRN2", target_bir_lowering=False, num_devices=1)
    args = [nc.dram_tensor(k, a.shape, F32, kind="ExternalInput").ap() for k, a in arrays.items()]
    out = nc.dram_tensor("out", (G, P, N), F32, kind="ExternalOutput").ap()
    build(nc, *args, out)
    got = run_bass_kernel_spmd(nc, [arrays], core_ids=[0]).results[0]["out"]
    return got.reshape(B, C, T, V)
```

```python
from contextlib import ExitStack

import numpy as np

import concourse.bass as bass
from concourse import mybir

F32 = mybir.dt.float32
BF16 = mybir.dt.bfloat16
I32 = mybir.dt.int32
ALU = mybir.AluOpType
ACT = mybir.ActivationFunctionType

B, C, T, V = 32, 32, 16, 25
N = T * V
NB = 4
G = B // NB
PAIRS = G // 2
P = NB * C
BR, CB, K = 4, C // 4, 5
CH = C // 2
TT, MT = 4, 100
OUTER = (-2, -1, 1, 2)
PAD = 4 * V
BN_EPS = LN_EPS = 1e-5
L = 10
NC = N // L
UNROLL = 5
BANKS = (0, 1, 2, 3, 1)
COLS = G * NC
HALF = COLS // 2
PROB = NB * TT * N
RB = 8
TWO_ONES = float(np.frombuffer(np.uint32(0x3F803F80).tobytes(), np.float32)[0])
MEET = (2.0 ** -18) ** 2

COLUMNS = {}


def _place(at, *entries):
    for name, width in entries:
        COLUMNS[name] = (at, width)
        at += width
    return at


MIX_AT = _place(0, ("center", P), ("mean", P), ("wT", P), ("w", P), ("vT", P), ("avg4", P))
LATE_W = _place(MIX_AT, ("mix", P), ("branch", P), ("taps", 2 * P), ("middle", P), ("rotT", P), ("wqT", P),
                ("entT", P), ("wkT", P), ("wvT", P), ("sel", C))
KEEP_AT = _place(LATE_W, ("al", MT), ("alT", MT), ("intraT", MT), ("interT", MT), ("flatT", MT))
ALL_W = _place(KEEP_AT, ("ident", P), ("bn_g", 3), ("bn_b", 3), ("bn_m", 3), ("bn_v", 3), ("keep", 3), ("pass", 3),
               ("not_first", 1), ("third", 1), ("gamma", 1), ("beta", 1), ("eps", 1), ("ones", C))
assert KEEP_AT - MIX_AT >= NB * N


def build(nc, x_tok, x, consts, out):
    with ExitStack() as ctx:
        def sb(name, shape, dt=F32):
            return ctx.enter_context(nc.sbuf_tensor(name, shape, dt))

        def sem(name):
            return ctx.enter_context(nc.semaphore(name))

        cst = sb("cst", [P, ALL_W])

        def c_(name, rows=P):
            o, w = COLUMNS[name]
            return cst[0:rows, o:o + w]

        t0 = sb("t0", [P, G, N])
        vst = sb("vst", [MT, G, 4 * P])
        stacks = sb("stacks", [P, 4 * B * N // 2])
        arena = sb("arena", [P, 2 * PROB + N])
        vb = sb("vb", [MT, 2, 4 * P])
        prep = sb("prep", [P, 2 * P + 5 * MT])
        small = sb("small", [P, 64])
        stat = sb("stat", [P, G, 6])
        wsc = sb("wsc", [P, P])
        diag = sb("diag", [P, P])
        flag = sb("flag", [1, 1], I32)
        ps = ctx.enter_context(nc.psum_tensor("ps", [P, 8, 512], F32))
        sq = [sb(f"sq{h}", [P, N])[:, :] for h in range(2)]

        aq = prep[:, 0:2 * P].rearrange("p (k n) -> p k n", k=2)
        mlo = prep[0:MT, 2 * P:2 * P + 2 * MT].rearrange("p (k n) -> p k n", k=2)
        t2, ia, dd = (prep[0:MT, 2 * P + n * MT:2 * P + n * MT + MT] for n in (2, 3, 4))

        def stack(n):
            w = B * N // 2
            return stacks[:, n * w:(n + 1) * w].bitcast(BF16).rearrange("p (b n) -> p b n", n=N)

        ka, kb, qa, qb = (stack(n) for n in range(4))

        cut = [0]

        def piece(width, dt=F32):
            a = arena[:, cut[0]:cut[0] + width]
            cut[0] += width
            return a if dt == F32 else a.bitcast(dt)

        xks = piece(2 * TT * P).rearrange("p (g n) -> p g n", g=2)
        xk = [xks[:, h, :] for h in range(2)]
        y0 = [piece(N) for _ in range(2)]
        y4 = [piece(N) for _ in range(2)]
        zp = [piece(N + 2 * PAD) for _ in range(2)]
        tap_in = [[piece(N) for _ in range(2)] for _ in range(2)]
        mx, ts = y0, y4
        assert cut[0] <= PROB
        cut[0] = PROB
        rstd = [piece(N) for _ in range(2)]
        xl = [piece(N) for _ in range(2)]
        kp, qp = ([piece(3 * N // 2, BF16).rearrange("p (s n) -> p s n", n=N) for _ in range(2)]
                  for _ in range(2))
        rk = [piece(N) for _ in range(2)]
        rq = [piece(N) for _ in range(2)]
        es = piece(N)
        ep = piece(3 * N // 2, BF16).rearrange("p (s n) -> p s n", n=N)
        sqk, sqq = sq, rstd
        assert cut[0] <= 2 * PROB + N
        prob = [arena[0:MT, h * PROB:(h + 1) * PROB].rearrange("p (b k n) -> p b k n", b=NB, k=TT)
                for h in range(2)]
        rden = arena[:, 2 * PROB:2 * PROB + N]
        psum = cst[0:MT, MIX_AT:MIX_AT + NB * N].rearrange("p (b n) -> p b n", b=NB)
        nrm, sq2 = sq
        rs2 = prep[:, 0:N]

        xl2 = stacks[:, 0:G * 2 * N].rearrange("p (g n) -> p g n", g=G)

        def xs(g):
            return xl2[:, bass.ds(g, 1), 0:N].rearrange("p o n -> p (o n)")

        at_y = B * N // 2
        yb = stacks[:, at_y:at_y + (L + 1) * COLS].rearrange("p (s g c) -> p s g c", s=L + 1, g=G)
        at_y += (L + 1) * COLS
        ys, yd = (stacks[:, at_y + n * COLS:at_y + (n + 1) * COLS].rearrange("p (g c) -> p g c", g=G)
                  for n in range(2))
        at_y += 2 * COLS
        outs = stacks[:, at_y:at_y + G * N].rearrange("p (g n) -> p g n", n=N)

        dka, dqa, dkb, dqb = (nc.dram_tensor(name, [G, P, n * N], BF16, kind="Internal").ap()
                              for name, n in (("dka", 4), ("dqa", 4), ("dkb", 2), ("dqb", 2)))
        de = nc.dram_tensor("de", [PAIRS, P, N], BF16, kind="Internal").ap()

        def col(n, w=1, rows=P):
            return small[0:rows, n:n + w]

        rowsum, dmax, dln, dcol = (col(n, 1, MT) for n in range(4))
        bn_ln, bn_r, bn_s, bn_ms, bn_h = (col(4 + 3 * n, 3) for n in range(5))
        bn_s2, bn_h2 = col(19, 3), col(22, 3)
        mv, mm, tot, m2, vv, lnv, rsv, scl, msc, shf, okc = (
            col(25, 2), col(27, 2), col(29, 2), *(col(n) for n in range(31, 39)))
        S_GC, S_Z, S_POST = 0, 1, 2
        K_AT, Q_AT = (0, 1, 2), (1, 2, 0)

        early_in, late_in, x_tok_in, x_in, one_rows, e_rows_in, e_stored, out_done = (
            sem(n) for n in ("early_in", "late_in", "x_tok_in", "x_in", "one_rows", "e_rows_in",
                             "e_stored", "out_done"))
        kq_stored = [sem("kq_stored0"), sem("kq_stored1")]
        stack_in = [sem("stack_in0"), sem("stack_in1")]
        zeroed, abs_done, dve_c, act_c, pe_c, prep_done = (
            sem(n) for n in ("zeroed", "abs_done", "dve_c", "act_c", "pe_c", "prep_done"))
        (v_mixed, y0_ready, mixed, y_ready, branched, zp_ready, mx_ready, u_ready, u_act, pooled, tapped, ts_ready,
         t0_ready) = (
            sem(n) for n in ("v_mixed", "y0_ready", "mixed", "y_ready", "branched", "zp_ready", "mx_ready",
                             "u_ready", "u_act", "pooled", "tapped", "ts_ready", "t0_ready"))
        (centered, sq_ready, var_done, ln_ready, rstd_ready, xl_ready, kq_done, k1_ready, q1_ready, rk_ready,
         rq_ready, seconds, parts_ready, v_done, v_ready, e_done, es_ready, e_step, e_ready) = (
            sem(n) for n in ("centered", "sq_ready", "var_done", "ln_ready", "rstd_ready", "xl_ready", "kq_done",
                             "k1_ready", "q1_ready", "rk_ready", "rq_ready", "seconds", "parts_ready", "v_done",
                             "v_ready", "e_done", "es_ready", "e_step", "e_ready"))
        (s_done, e1_done, p_ready, part_sum, psum_ready, sums_done, vb_ready, pv_done, rden_ready, nrm_ready,
         t1_ready) = (
            sem(n) for n in ("s_done", "e1_done", "p_ready", "part_sum", "psum_ready", "sums_done", "vb_ready",
                             "pv_done", "rden_ready", "nrm_ready", "t1_ready"))
        centered2, sq2_ready, var2_done, ln2_ready, rs2_ready, xl2_ready, wx_done, stat_ready = (
            sem(n) for n in ("centered2", "sq2_ready", "var2_done", "ln2_ready", "rs2_ready", "xl2_ready",
                             "wx_done", "stat_ready"))
        bn_c, bn_pe, bn_act, wsc_ready, start_ok, cmp_c, cmp_pe, flag_ok, added = (
            sem(n) for n in ("bn_c", "bn_pe", "bn_act", "wsc_ready", "start_ok", "cmp_c", "cmp_pe", "flag_ok",
                             "added"))
        pre = [sem("pre0"), sem("pre1")]
        y_ok = [sem("y_ok0"), sem("y_ok1")]
        CREDIT = 2
        CREDIT1 = 1
        CREDIT_DMA = 16
        OUT_G = 2

        def by_step(t, s):
            return t[:, :, :].rearrange("p g (c s) -> p s (g c)", s=L)[:, bass.ds(s, 1), :].rearrange("p o n -> p (o n)")

        ACT_TAPS = (2, 3)

        def tap_input(par, j, k):
            o = PAD + V * OUTER[k] * (j + 1)
            return tap_in[par][j][C * k:C * k + C, :], zp[par][C * j:C * j + C, o:o + N]

        def at(t, g):
            return t[:, bass.ds(g, 1), :].rearrange("p o n -> p (o n)")

        block = ctx.enter_context(nc.Block())

        @block.sync
        def _(sp):
            sp.dma_start(cst[:, LATE_W:], consts[:, LATE_W:]).then_inc(early_in, 16)

            def load_tokens(i):
                sp.dma_start(xks[0:MT], x_tok[2 * i:2 * i + 2].rearrange("g p n -> p g n")).then_inc(x_tok_in, 16)

            def block_in(dst, first, rows, src, g, done):
                sp.dma_start(dst[first:first + rows, bass.ds(NB * g, NB), :], src).then_inc(done, 16)

            def stack(i):
                later = not isinstance(i, int) or i > 0
                for par in range(2):
                    g = 2 * i + par
                    sp.wait_ge(parts_ready, 2 * g + 2)
                    kpp, qpp = kp[par], qp[par]
                    for scratch, lo, hi, part in (
                            (dka, 0, 2, kpp[:, 0:1].to_broadcast([P, 2, N])),
                            (dka, 2, 4, kpp[:, 1:2].to_broadcast([P, 2, N])),
                            (dqa, 0, 2, qpp[:, 1:3]), (dqa, 2, 4, qpp[:, 1:3]),
                            (dkb, 0, 2, kpp[:, 0:3:2]),
                            (dqb, 0, 2, qpp[:, 0:2])):
                        sp.dma_start(scratch[bass.ds(g, 1), :, N * lo:N * hi].rearrange("o p (s n) -> (o p) s n", n=N),
                                     part).then_inc(kq_stored[par], 16)
                sp.wait_ge(e_ready, i + 1 + CREDIT1)
                sp.dma_start(de[bass.ds(i, 1)].rearrange("o p n -> p (o n)"), ep[:, 2, :]).then_inc(e_stored, 16)
                for par in range(2):
                    g = 2 * i + par
                    if later:
                        sp.wait_ge(stack_in[par], 16 * 4 * i)
                    sp.wait_ge(kq_stored[par], 96 * i + 96 + CREDIT_DMA)
                    for dst, scratch, n in ((ka, dka, 4), (qa, dqa, 4), (kb, dkb, 2), (qb, dqb, 2)):
                        block_in(dst, 0, n * C, scratch[bass.ds(g, 1)].rearrange(
                            "o (b c) (s n) -> (c s) (o b) n", b=NB, n=N), g, stack_in[par])
                if later:
                    sp.wait_ge(e_rows_in, 16 * 4 * i)
                sp.wait_ge(e_stored, 16 * i + 16 + CREDIT_DMA)
                rows = de[bass.ds(i, 1)].rearrange("o (g h b r) n -> g h r (o b) n", g=2, h=2, b=NB)
                for par in range(2):
                    block_in(kb, 2 * C, 3, rows[par, 0, 0:3], 2 * i + par, e_rows_in)
                    block_in(qb, 2 * C + 3, 3, rows[par, 1, 0:3], 2 * i + par, e_rows_in)

            load_tokens(0)
            sp.dma_start(t0[:, :, :], x.rearrange("g p n -> p g n")).then_inc(x_in, 16)
            for s in (*kq_stored, e_stored):
                sp.sem_inc(s, CREDIT_DMA)
            sp.wait_ge(zeroed, 6)
            sp.dma_start(kb[67:70, :, :], qb[64:67, :, :]).then_inc(one_rows, 16)
            for i in range(PAIRS - 1):
                sp.wait_ge(v_mixed, 2 * i + 2)
                load_tokens(i + 1)
                if i >= 2:
                    stack(i - 2)
            with sp.Fori(PAIRS - 3, PAIRS) as i:
                stack(i)
            def store_output(sums):
                sp.wait_ge(added, L * sums)
                for g in range(0, G, OUT_G):
                    sp.dma_start(out[g:g + OUT_G].rearrange("g p n -> p g n"),
                                 outs[:, g:g + OUT_G, :]).then_inc(out_done, 16)
                sp.wait_ge(out_done, 16 * (G // OUT_G) * sums)

            store_output(1)
            sp.wait_ge(flag_ok, 1)
            with sp.If(sp.value_load(flag[0:1, 0:1], min_val=0, max_val=1) != 0):
                store_output(2)

        @block.gpsimd
        def _(pool):
            fills = [(zp[h][:, o:o + PAD], 0.0) for h in range(2) for o in (0, PAD + N)]
            fills += [(t[64:96, :, :].rearrange("p b n -> p (b n)").bitcast(F32), v) for t, v in ((kb, 0.0), (qb, TWO_ONES))]
            for n, (t, v) in enumerate(fills):
                if n:
                    pool.wait_ge(zeroed, n)
                nc.gpsimd.memset(t, v).then_inc(zeroed, 1)
            pool.wait_ge(zeroed, len(fills))
            pool.wait_ge(early_in, 16)
            with pool.Fori(0, PAIRS) as i:
                a, b, f = (ep[:, s, :] for s in range(3))
                pool.wait_ge(es_ready, 2 * i + 2 + CREDIT)
                pool.wait_ge(e_stored, 16 * i + CREDIT_DMA)
                nc.gpsimd.tensor_tensor(a, es, c_("not_first").to_broadcast([P, N]), ALU.mult).then_inc(e_step, 1)
                pool.wait_ge(e_step, 3 * i + 1)
                nc.gpsimd.tensor_tensor(es, es, a, ALU.add).then_inc(e_step, 1)
                pool.wait_ge(e_step, 3 * i + 2)
                nc.gpsimd.tensor_tensor(b, es, c_("third").to_broadcast([P, N]), ALU.mult).then_inc(e_step, 1)
                pool.wait_ge(e_step, 3 * i + 3)
                nc.gpsimd.tensor_tensor(f, es, b, ALU.add).then_inc(e_ready, 1)

            def values(g, par):
                nc.gpsimd.tensor_copy(vb[:, par, :], at(vst, g)).then_inc(vb_ready, 1)

            def residual(g):
                pool.wait_ge(nrm_ready, g + 1)
                nc.gpsimd.tensor_tensor(at(t0, g), at(t0, g), nrm, ALU.add).then_inc(t1_ready, 1)

            pool.wait_ge(v_ready, G + CREDIT)
            for par in range(2):
                values(par, par)
            with pool.Fori(0, PAIRS - 1) as i:
                for par in range(2):
                    residual(2 * i + par)
                    values(2 * i + 2 + par, par)
            residual(G - 2)

        @block.scalar
        def _(act):
            act.dma_start(cst[:, 0:LATE_W], consts[:, 0:LATE_W]).then_inc(late_in, 16)
            nc.scalar.preload_act_table_set("natural_log_exp_and_others")
            act.wait_ge(early_in, 16)
            nc.scalar.activation(dd, c_("al", MT), ACT.Abs, accum_out=rowsum)
            nc.scalar.activation(t2, c_("alT", MT), ACT.Abs).then_inc(abs_done, 1)
            nc.scalar.activation(bn_ln, c_("bn_v"), ACT.Ln, bias=c_("eps")).then_inc(act_c, 1)
            act.wait_ge(act_c, 1)
            nc.scalar.activation(bn_r, bn_ln, ACT.Exp, scale=-0.5).then_inc(act_c, 1)
            act.wait_ge(dve_c, 1)
            nc.scalar.activation(dln, dmax, ACT.Ln).then_inc(act_c, 1)
            act.wait_ge(act_c, 3)
            nc.scalar.activation(dcol, dln, ACT.Exp, scale=-0.5).then_inc(act_c, 1)
            act.wait_ge(prep_done, 1)

            def y_relu(i):
                for par in range(2):
                    act.wait_ge(mixed, 2 * i + par + 1)
                    nc.scalar.activation(y4[par], ps[:, 2 * par + 1, 0:N], ACT.Relu, bias=bn_h2[:, S_GC:S_GC + 1],
                                         scale=bn_s2[:, S_GC:S_GC + 1]).then_inc(y_ready, 1)

            def branches(i):
                for par in range(2):
                    act.wait_ge(branched, 2 * i + par + 1)
                    for lo, hi, f in ((0, 96, ACT.Relu), (96, P, ACT.Identity)):
                        last = nc.scalar.activation(zp[par][lo:hi, PAD:PAD + N], ps[lo:hi, 2 * par, 0:N], f,
                                                    bias=bn_h2[lo:hi, S_Z:S_Z + 1], scale=bn_s2[lo:hi, S_Z:S_Z + 1])
                    last.then_inc(zp_ready, 1)
                for par in range(2):
                    act.wait_ge(zp_ready, 2 * i + par + 1)
                    for k in ACT_TAPS:
                        last = nc.scalar.copy(*tap_input(par, 1, k))
                    last.then_inc(u_act, 1)

            def t_relu(i):
                for par in range(2):
                    g = 2 * i + par
                    act.wait_ge(ts_ready, g + 1)
                    nc.scalar.activation(at(t0, g), ts[par], ACT.Relu,
                                         bias=bn_h2[:, S_POST:S_POST + 1]).then_inc(t0_ready, 1)

            def squares(i):
                for par in range(2):
                    act.wait_ge(centered, 2 * i + par + 1)
                    nc.scalar.activation(sq[par], ps[:, 4 + 2 * par, 0:N], ACT.Square).then_inc(sq_ready, 1)

            def inverse_roots(i):
                for par in range(2):
                    act.wait_ge(var_done, 2 * i + par + 1)
                    nc.scalar.activation(rstd[par], ps[:, 5 + 2 * par, 0:N], ACT.Ln,
                                         bias=c_("eps")).then_inc(ln_ready, 1)
                for par in range(2):
                    act.wait_ge(ln_ready, 2 * i + par + 1)
                    nc.scalar.activation(rstd[par], rstd[par], ACT.Exp, scale=-0.5).then_inc(rstd_ready, 1)

            def kq_firsts(i):
                for par in range(2):
                    g = 2 * i + par
                    act.wait_ge(kq_done, g + 1)
                    act.wait_ge(kq_stored[par], 96 * i + CREDIT_DMA)
                    for parts, slot, s, n, ready in ((kp, K_AT[0], sqk, 4, k1_ready), (qp, Q_AT[0], sqq, 5, q1_ready)):
                        nc.scalar.copy(parts[par][:, slot, :], ps[:, n + 2 * par, 0:N])
                        nc.scalar.activation(s[par], ps[:, n + 2 * par, 0:N], ACT.Square).then_inc(ready, 1)

            def v_and_squares(i):
                for par in range(2):
                    g = 2 * i + par
                    act.wait_ge(v_done, g + 1)
                    nc.scalar.copy(at(vst, g), ps[0:MT, 4 + 2 * par, :]).then_inc(v_ready, 1)
                    act.wait_ge(e_done, g + 1)
                    act.wait_ge(e_ready, i + 1)
                    lo, hi = 2 * C * par, 2 * C * (par + 1)
                    nc.scalar.copy(es[lo:hi], ps[lo:hi, 5 + 2 * par, 0:N]).then_inc(es_ready, 1)

            y_relu(0)
            branches(0)
            t_relu(0)
            with act.Fori(0, PAIRS - 1) as i:
                squares(i)
                y_relu(i + 1)
                inverse_roots(i)
                branches(i + 1)
                kq_firsts(i)
                t_relu(i + 1)
                v_and_squares(i)
            def inner(g, par, u):
                act.wait_ge(s_done, 8 * g + u + 1)
                nc.scalar.activation(prob[par][:, u // 2, 2 * (u % 2):2 * (u % 2) + 2, :],
                                     ps[0:MT, 2 * (u % 2):2 * (u % 2) + 2, 0:N], ACT.Exp,
                                     scale=2.0).then_inc(e1_done, 1)

            def outer(g, par, u):
                act.wait_ge(e1_done, 8 * g + u + 1)
                p = prob[par][:, u // 2, 2 * (u % 2):2 * (u % 2) + 2, :]
                nc.scalar.activation(p, p, ACT.Exp).then_inc(p_ready, 1)

            def norm2(g, step):
                if step == 0:
                    act.wait_ge(centered2, g + 1)
                    nc.scalar.activation(sq2, ps[:, 6, 0:N], ACT.Square).then_inc(sq2_ready, 1)
                elif step == 1:
                    act.wait_ge(var2_done, g + 1)
                    nc.scalar.activation(rs2, ps[:, 7, 0:N], ACT.Ln, bias=c_("eps")).then_inc(ln2_ready, 1)
                else:
                    act.wait_ge(ln2_ready, g + 1)
                    nc.scalar.activation(rs2, rs2, ACT.Exp, scale=-0.5).then_inc(rs2_ready, 1)

            def weights(g, par):
                first = isinstance(g, int)
                if not first:
                    act.wait_ge(pv_done, g - 1)
                for u in range(8):
                    if first and g == 1 and u == 2:
                        for h in range(2):
                            act.wait_ge(kq_stored[h], 96 * PAIRS + CREDIT_DMA)
                    if first and g == 1 and u == 6:
                        act.wait_ge(e_stored, 16 * PAIRS + CREDIT_DMA)
                    inner(g, par, u)
                    if u:
                        outer(g, par, u - 1)
                    elif not first or g:
                        outer(g - 1, 1 - par, 7)
                    if not first and u in (1, 3, 4):
                        norm2(g - 2, (1, 3, 4).index(u))

            for step, first, end in ((squares, 0, 2), (inverse_roots, 2, 3), (kq_firsts, 3, 5), (v_and_squares, 5, 8)):
                step(PAIRS - 1)
                for u in range(first, end):
                    inner(0, 0, u)
                    if u:
                        outer(0, 0, u - 1)
            weights(1, 1)
            with act.Fori(1, PAIRS) as i:
                for par in range(2):
                    weights(2 * i + par, par)
            outer(G - 1, 1, 7)
            norm2(G - 2, 0)
            norm2(G - 2, 1)
            norm2(G - 2, 2)
            for step in range(3):
                norm2(G - 1, step)
            act.wait_ge(bn_c, 4)
            nc.scalar.activation(lnv, vv, ACT.Ln, bias=c_("eps")).then_inc(bn_act, 1)
            act.wait_ge(bn_act, 1)
            nc.scalar.activation(rsv, lnv, ACT.Exp, scale=-0.5).then_inc(bn_act, 1)

            nc.scalar.preload_act_table_set("sigmoid_and_others")
            act.wait_ge(wsc_ready, 1)
            act.wait_ge(bn_c, 8)

            def steps(base, count):
                with act.Fori(0, count // UNROLL) as i:
                    for k, bank in enumerate(BANKS):
                        s = UNROLL * i + k
                        for h in range(2):
                            act.wait_ge(pre[h], base + s + 1)
                            nc.scalar.activation(
                                yb[:, bass.ds(s + 1, 1), 4 * h:4 * h + 4, :].rearrange("p o g c -> p (o g c)"),
                                ps[:, 4 * h + bank, 0:HALF], ACT.Sigmoid, bias=shf).then_inc(y_ok[h], 1)

            for sweep in range(2):
                steps(L * sweep, L)
            act.wait_ge(flag_ok, 1)
            with act.If(act.value_load(flag[0:1, 0:1], min_val=0, max_val=1) != 0):
                with act.Fori(0, NC - 1) as k:
                    steps(2 * L + L * k, L)

        @block.vector
        def _(dve):
            count = [0]

            def link(ins, s=dve_c, c=count):
                c[0] += 1
                ins.then_inc(s, 1)
                dve.wait_ge(s, c[0])

            dve.wait_ge(early_in, 16)
            dve.wait_ge(abs_done, 1)
            link(nc.vector.tensor_scalar(dmax, rowsum, 1e-6, None, ALU.max))
            dve.wait_ge(act_c, 4)
            link(nc.vector.tensor_scalar(dd, c_("ident", MT)[:, 0:MT], dcol, None, ALU.mult))
            link(nc.vector.tensor_tensor(bn_s, bn_r, c_("bn_g"), ALU.mult))
            link(nc.vector.tensor_tensor(bn_ms, bn_s, c_("bn_m"), ALU.mult))
            link(nc.vector.tensor_tensor(bn_h, c_("bn_b"), bn_ms, ALU.subtract))
            link(nc.vector.tensor_tensor(bn_h2, bn_h, c_("keep"), ALU.mult))
            link(nc.vector.tensor_tensor(bn_s, bn_s, c_("keep"), ALU.mult))
            link(nc.vector.tensor_tensor(bn_s2, bn_s, c_("pass"), ALU.add))
            dve.wait_ge(pe_c, 1)
            link(nc.vector.scalar_tensor_tensor(out=ia, in0=ps[0:MT, 2, 0:MT], scalar=dcol,
                                                in1=c_("ident", MT)[:, 0:MT], op0=ALU.mult, op1=ALU.add))
            dve.wait_ge(pe_c, 3)
            nc.vector.tensor_copy(mlo[:, 0, :], ps[0:MT, 2, 0:MT])
            link(nc.vector.tensor_copy(t2, ps[0:MT, 3, 0:MT]))
            dve.wait_ge(pe_c, 6)
            nc.vector.tensor_copy(mlo[:, 1, :], ps[0:MT, 0, 0:MT])
            nc.vector.tensor_copy(aq[:, 0, :], ps[:, 6, 0:P])
            nc.vector.tensor_copy(aq[:, 1, :], ps[:, 7, 0:P]).then_inc(prep_done, 1)
            dve.wait_ge(zeroed, 4)

            def y_copy(i):
                for par in range(2):
                    dve.wait_ge(v_mixed, 2 * i + par + 1)
                    nc.vector.tensor_copy(y0[par], ps[:, 2 * par, 0:N]).then_inc(y0_ready, 1)

            def tap_inputs(i):
                for par in range(2):
                    g = 2 * i + par
                    z = zp[par]
                    dve.wait_ge(zp_ready, g + 1)
                    nc.vector.tensor_tensor(mx[par][64:96, :], z[64:96, PAD - V:PAD - V + N],
                                            z[64:96, PAD + V:PAD + V + N], ALU.max).then_inc(mx_ready, 1)
                    for j in range(2):
                        for k in range(len(OUTER)):
                            if j == 0 or k not in ACT_TAPS:
                                last = nc.vector.tensor_copy(*tap_input(par, j, k))
                        last.then_inc(u_ready, 1)
                    dve.wait_ge(mx_ready, g + 1)
                    mid = z[64:96, PAD:PAD + N]
                    nc.vector.tensor_tensor(mid, mid, mx[par][64:96, :], ALU.max).then_inc(pooled, 1)

            def add_x(i):
                for par in range(2):
                    dve.wait_ge(tapped, 2 * i + par + 1)
                    nc.vector.scalar_tensor_tensor(out=ts[par], in0=ps[:, 2 * par + 1, 0:N],
                                                   scalar=bn_s2[:, S_POST:S_POST + 1], in1=at(t0, 2 * i + par),
                                                   op0=ALU.mult, op1=ALU.add).then_inc(ts_ready, 1)

            def norm(i):
                for par in range(2):
                    g = 2 * i + par
                    dve.wait_ge(rstd_ready, g + 1)
                    nc.vector.tensor_tensor(xl[par], ps[:, 4 + 2 * par, 0:N], rstd[par],
                                            ALU.mult).then_inc(xl_ready, 1)

            def rests(i):
                for par in range(2):
                    g = 2 * i + par
                    dve.wait_ge(k1_ready, g + 1)
                    nc.vector.tensor_tensor(rk[par], ps[:, 4 + 2 * par, 0:N], kp[par][:, K_AT[0], :],
                                            ALU.subtract).then_inc(rk_ready, 1)
                    dve.wait_ge(q1_ready, g + 1)
                    nc.vector.tensor_tensor(rq[par], ps[:, 5 + 2 * par, 0:N], qp[par][:, Q_AT[0], :],
                                            ALU.subtract).then_inc(rq_ready, 1)

            def parts(i):
                for par in range(2):
                    g = 2 * i + par
                    for n, (r, p, slots) in enumerate(((rk, kp, K_AT), (rq, qp, Q_AT))):
                        dve.wait_ge((rk_ready, rq_ready)[n], g + 1)
                        nc.vector.tensor_copy(p[par][:, slots[1], :], r[par]).then_inc(seconds, 1)
                    for n, (r, p, slots) in enumerate(((rk, kp, K_AT), (rq, qp, Q_AT))):
                        dve.wait_ge(seconds, 2 * g + n + 1)
                        nc.vector.tensor_tensor(p[par][:, slots[2], :], r[par], p[par][:, slots[1], :],
                                                ALU.subtract).then_inc(parts_ready, 1)

            dve.wait_ge(x_in, 16)
            y_copy(0)
            tap_inputs(0)
            add_x(0)
            with dve.Fori(0, PAIRS - 1) as i:
                y_copy(i + 1)
                norm(i)
                tap_inputs(i + 1)
                rests(i)
                add_x(i + 1)
                parts(i)
            norm(PAIRS - 1)
            rests(PAIRS - 1)
            parts(PAIRS - 1)

            def add_tiles(g, par, u):
                p = prob[par][:, u // 2, :, :]
                dst = psum[:, u // 2, :]
                n = 12 * g + 3 * (u // 2)
                dve.wait_ge(p_ready, 8 * g + u + 1)
                if u % 2 == 0:
                    nc.vector.tensor_tensor(dst, p[:, 0, :], p[:, 1, :], ALU.add).then_inc(part_sum, 1)
                else:
                    for k in (2, 3):
                        dve.wait_ge(part_sum, n + k - 1)
                        nc.vector.tensor_tensor(dst, dst, p[:, k, :], ALU.add).then_inc(part_sum, 1)

            def reciprocals(g, first=False):
                dve.wait_ge(sums_done, g + 1)
                if first:
                    dve.wait_ge(e_stored, 16 * PAIRS + CREDIT_DMA)
                else:
                    dve.wait_ge(nrm_ready, g)
                nc.vector.reciprocal(rden, ps[:, 5, 0:N]).then_inc(rden_ready, 1)

            def quotient(g, first=False):
                dve.wait_ge(pv_done, g + 1)
                dve.wait_ge(rden_ready, g + 1)
                if not first:
                    dve.wait_ge(t1_ready, g)
                nc.vector.tensor_tensor(nrm, ps[:, 4, 0:N], rden, ALU.mult).then_inc(nrm_ready, 1)

            def norm2(g):
                dve.wait_ge(rs2_ready, g + 1)
                nc.vector.tensor_tensor(xs(g).rearrange("p (s c) -> p s c", s=L),
                                        ps[:, 6, 0:N].rearrange("p (c s) -> p s c", s=L),
                                        rs2.rearrange("p (c s) -> p s c", s=L), ALU.mult).then_inc(xl2_ready, 1)

            def stats(g):
                dve.wait_ge(wx_done, g + 1)
                nc.vector.bn_stats(at(stat, g), ps[:, 7, 0:N]).then_inc(stat_ready, 1)

            def attend(g, par, products, norms):
                if products:
                    dve.wait_ge(sums_done, g)
                for u in range(8):
                    if u == 7 and norms:
                        stats(g - 2)
                    add_tiles(g, par, u)
                    if products and u == 1:
                        reciprocals(g - 1, first=not norms)
                    if products and u == 4:
                        quotient(g - 1, first=not norms)
                    if norms and u == 3:
                        norm2(g - 2)

            dve.wait_ge(e_done, G)
            attend(0, 0, False, False)
            attend(1, 1, True, False)
            with dve.Fori(1, PAIRS) as i:
                for par in range(2):
                    attend(2 * i + par, par, True, True)
            norm2(G - 2)
            reciprocals(G - 1)
            stats(G - 2)
            quotient(G - 1)
            dve.wait_ge(nrm_ready, G)
            nc.vector.tensor_tensor(t0[:, G - 1, :], t0[:, G - 1, :], nrm, ALU.add).then_inc(t1_ready, 1)
            norm2(G - 1)
            stats(G - 1)

            bc = [0]

            def blink(ins):
                link(ins, bn_c, bc)

            dve.wait_ge(stat_ready, G + CREDIT1)
            blink(nc.vector.bn_aggr(mv, stat[:, :, :].rearrange("p g s -> p (g s)")))
            blink(nc.vector.tensor_tensor(m2, mv[:, 0:1], mv[:, 0:1], ALU.mult))
            nc.vector.tensor_copy(mm[:, 0:1], mv[:, 0:1])
            blink(nc.vector.tensor_tensor(mm[:, 1:2], mv[:, 1:2], m2, ALU.add))
            dve.wait_ge(bn_pe, 1)
            nc.vector.tensor_copy(tot, ps[:, 5, 0:2]).then_inc(cmp_c, 1)
            dve.wait_ge(cmp_c, 1)
            nc.vector.tensor_tensor(m2, tot[:, 0:1], tot[:, 0:1], ALU.mult).then_inc(cmp_c, 1)
            dve.wait_ge(cmp_c, 2)
            blink(nc.vector.tensor_tensor(vv, tot[:, 1:2], m2, ALU.subtract))
            dve.wait_ge(bn_act, 2)
            blink(nc.vector.tensor_tensor(scl, rsv, c_("gamma"), ALU.mult))
            blink(nc.vector.tensor_scalar(diag[:, :], c_("ident"), scl, None, ALU.mult))
            blink(nc.vector.tensor_tensor(msc, tot[:, 0:1], scl, ALU.mult))
            blink(nc.vector.tensor_tensor(shf, c_("beta"), msc, ALU.subtract))
            nc.vector.memset(yb[:, 0, :, :], 0.0).then_inc(start_ok, 1)
            dve.wait_ge(bn_pe, 2)
            nc.vector.tensor_copy(wsc[:, :], ps[:, 6, 0:P]).then_inc(wsc_ready, 1)

            def chain(base):
                for h in range(2):
                    dve.wait_ge(y_ok[h], base + CREDIT)
                nc.vector.tensor_copy(yb[:, 0, :, 1:NC], yb[:, L, :, 0:NC - 1]).then_inc(start_ok, 1)

            for h in range(2):
                dve.wait_ge(y_ok[h], L + CREDIT)
            nc.vector.tensor_copy(ys, yb[:, L, :, :]).then_inc(cmp_c, 1)
            chain(L)
            def add_residual():
                with dve.Fori(0, L // UNROLL) as i:
                    for k in range(UNROLL):
                        j = UNROLL * i + k
                        for h in range(2):
                            dve.wait_ge(y_ok[h], L + j + 1 + CREDIT)
                        nc.vector.tensor_tensor(by_step(outs, j), by_step(t0, j),
                                                yb[:, bass.ds(j + 1, 1), :, :].rearrange("p o g c -> p (o g c)"),
                                                ALU.add).then_inc(added, 1)

            add_residual()
            dve.wait_ge(cmp_c, 3)
            nc.vector.tensor_tensor(yd, yb[:, L, :, :], ys, ALU.subtract).then_inc(cmp_c, 1)
            dve.wait_ge(cmp_c, 4)
            nc.vector.tensor_tensor(ys, yd, yd, ALU.mult).then_inc(cmp_c, 1)
            dve.wait_ge(cmp_c, 5)
            nc.vector.tensor_scalar(yd, ys, MEET, None, ALU.is_le, ALU.add, accum_out=okc).then_inc(cmp_c, 1)
            dve.wait_ge(cmp_pe, 1)
            nc.vector.tensor_scalar(flag[0:1, 0:1], ps[0:1, 7, 0:1], float(P * COLS), None,
                                    ALU.not_equal).then_inc(flag_ok, 1)
            dve.wait_ge(flag_ok, 1)
            with dve.If(dve.value_load(flag[0:1, 0:1], min_val=0, max_val=1) != 0):
                with dve.Fori(0, NC - 1) as k:
                    chain(2 * L + L * k)
                for h in range(2):
                    dve.wait_ge(y_ok[h], 2 * L + L * (NC - 1) + CREDIT)
                dve.wait_ge(out_done, 16 * (G // OUT_G))
                add_residual()

        @block.tensor
        def _(pe):
            mm_ = nc.tensor.matmul
            for s in (v_ready, es_ready, *y_ok):
                pe.sem_inc(s, CREDIT)
            for s in (e_ready, xl2_ready, stat_ready):
                pe.sem_inc(s, CREDIT1)
            pe.wait_ge(dve_c, 2)
            mm_(ps[0:MT, 2, 0:MT], t2, dd, start=True, stop=True).then_inc(pe_c, 1)
            pe.wait_ge(dve_c, 9)
            mm_(ps[0:MT, 2, 0:MT], c_("intraT", MT), ia, start=True, stop=True).then_inc(pe_c, 1)
            mm_(ps[0:MT, 3, 0:MT], c_("interT", MT), ia, start=True, stop=True).then_inc(pe_c, 1)
            pe.wait_ge(dve_c, 10)
            mm_(ps[0:MT, 0, 0:MT], c_("flatT", MT), t2, start=True, stop=True).then_inc(pe_c, 1)
            pe.wait_ge(late_in, 16)
            mm_(ps[:, 6, 0:P], c_("rotT"), c_("wqT"), start=True, stop=True).then_inc(pe_c, 1)
            mm_(ps[:, 7, 0:P], c_("entT"), c_("wkT"), start=True, stop=True).then_inc(pe_c, 1)
            pe.wait_ge(prep_done, 1)

            def mix_v(i):
                pe.wait_ge(x_tok_in, 16 * i + 16)
                for par in range(2):
                    if not isinstance(i, int):
                        pe.wait_ge(zp_ready, 2 * i + par - 1)
                    for tt in range(TT):
                        for h in range(2):
                            o = P * tt + NB * CH * h
                            last = mm_(ps[NB * CH * h:NB * CH * (h + 1), 2 * par, MT * tt:MT * tt + MT],
                                       xk[par][0:MT, o:o + NB * CH], mlo[:, h, :], start=True, stop=True,
                                       skip_group_check=True)
                    last.then_inc(v_mixed, 1)

            def mix_c(i):
                for par in range(2):
                    pe.wait_ge(y0_ready, 2 * i + par + 1)
                    if not isinstance(i, int):
                        pe.wait_ge(ts_ready, 2 * i + par - 1)
                    mm_(ps[:, 2 * par + 1, 0:N], c_("mix"), y0[par], start=True, stop=True).then_inc(mixed, 1)

            def branches(i):
                for par in range(2):
                    pe.wait_ge(y_ready, 2 * i + par + 1)
                    mm_(ps[:, 2 * par, 0:N], c_("branch"), y4[par], start=True, stop=True).then_inc(branched, 1)

            def taps(i):
                for par in range(2):
                    o = COLUMNS["taps"][0]
                    for j in range(2):
                        pe.wait_ge(u_ready, 2 * (2 * i + par) + j + 1)
                        if j:
                            pe.wait_ge(u_act, 2 * i + par + 1)
                        mm_(ps[:, 2 * par + 1, 0:N], cst[:, o + P * j:o + P * j + P], tap_in[par][j],
                            start=(j == 0), stop=False)
                    pe.wait_ge(pooled, 2 * i + par + 1)
                    mm_(ps[:, 2 * par + 1, 0:N], c_("middle"), zp[par][:, PAD:PAD + N],
                        start=False, stop=True).then_inc(tapped, 1)

            def center(i):
                for par in range(2):
                    g = 2 * i + par
                    pe.wait_ge(t0_ready, g + 1)
                    pe.wait_ge(v_ready, g + 1)
                    mm_(ps[:, 4 + 2 * par, 0:N], c_("center"), at(t0, g), start=True, stop=True).then_inc(centered, 1)

            def variance(i):
                for par in range(2):
                    g = 2 * i + par
                    pe.wait_ge(sq_ready, g + 1)
                    pe.wait_ge(es_ready, g + 1)
                    mm_(ps[:, 5 + 2 * par, 0:N], c_("mean"), sq[par], start=True, stop=True).then_inc(var_done, 1)

            def project_kq(i):
                for par in range(2):
                    pe.wait_ge(xl_ready, 2 * i + par + 1)
                    mm_(ps[:, 4 + 2 * par, 0:N], aq[:, 1, :], xl[par], start=True, stop=True)
                    mm_(ps[:, 5 + 2 * par, 0:N], aq[:, 0, :], xl[par], start=True, stop=True).then_inc(kq_done, 1)

            def project_v(i):
                for par in range(2):
                    g = 2 * i + par
                    pe.wait_ge(rk_ready, g + 1)
                    for tt in range(TT):
                        last = mm_(ps[0:MT, 4 + 2 * par, P * tt:P * tt + P], xl[par][:, MT * tt:MT * tt + MT],
                                   c_("wvT"), start=True, stop=True, skip_group_check=True)
                    last.then_inc(v_done, 1)
                    pe.wait_ge(rq_ready, g + 1)
                    for n, s in enumerate((sqk, sqq)):
                        o = 2 * C * par + C * n
                        last = mm_(ps[o:o + C, 5 + 2 * par, 0:N], c_("sel"), s[par], start=True, stop=True,
                                   skip_group_check=True)
                    last.then_inc(e_done, 1)

            mix_v(0)
            mix_c(0)
            branches(0)
            taps(0)
            with pe.Fori(0, PAIRS - 1) as i:
                mix_v(i + 1)
                center(i)
                mix_c(i + 1)
                variance(i)
                branches(i + 1)
                project_kq(i)
                taps(i + 1)
                project_v(i)

            def scores(g, u):
                if u >= 2 or not isinstance(g, int) or g > 0:
                    pe.wait_ge(e1_done, 8 * g + u - 1)
                for k in range(2):
                    o = MT * (2 * (u % 2) + k)
                    dst = ps[0:MT, 2 * (u % 2) + k, 0:N]
                    for kk, qq, rows, first in ((ka, qa, P, True), (kb, qb, 96, False)):
                        last = mm_(dst, kk[0:rows, bass.ds(NB * g + u // 2, 1), o:o + MT].rearrange("p o n -> p (o n)"),
                                   qq[0:rows, bass.ds(NB * g + u // 2, 1), :].rearrange("p o n -> p (o n)"),
                                   start=first, stop=not first)
                last.then_inc(s_done, 1)

            def sums(g, first):
                pe.wait_ge(part_sum, 12 * g + 12)
                if not first:
                    pe.wait_ge(rden_ready, g)
                for b in range(NB):
                    last = mm_(ps[C * b:C * b + C, 5, 0:N], c_("ones", MT), psum[:, b, :], start=True, stop=True,
                               skip_group_check=True)
                last.then_inc(sums_done, 1)

            def products(g, par, k, first):
                if k in (0, 2):
                    pe.wait_ge(p_ready, 8 * g + 7 + k // 2)
                if k == 0:
                    pe.wait_ge(vb_ready, g + 1)
                    if not first:
                        pe.wait_ge(nrm_ready, g)
                for b in range(NB):
                    last = mm_(ps[C * b:C * b + C, 4, 0:N], vb[:, par, P * k + C * b:P * k + C * b + C],
                               prob[par][:, b, k, :], start=(k == 0), stop=(k == TT - 1), skip_group_check=True)
                if k == TT - 1:
                    last.then_inc(pv_done, 1)

            def center2(g):
                pe.wait_ge(t1_ready, g + 1)
                pe.wait_ge(xl2_ready, g + 1)
                mm_(ps[:, 6, 0:N], c_("center"), at(t0, g), start=True, stop=True).then_inc(centered2, 1)

            def variance2(g):
                pe.wait_ge(sq2_ready, g + 1)
                pe.wait_ge(stat_ready, g + 1)
                mm_(ps[:, 7, 0:N], c_("mean"), sq2, start=True, stop=True).then_inc(var2_done, 1)

            def wx(g):
                pe.wait_ge(xl2_ready, g + 1 + CREDIT1)
                mm_(ps[:, 7, 0:N], c_("wT"), xs(g), start=True, stop=True).then_inc(wx_done, 1)

            def attend(g, par, prods, norms):
                for u in range(8):
                    scores(g, u)
                    if norms and u == 0:
                        center2(g - 2)
                    if prods and 1 <= u < 5:
                        products(g - 1, 1 - par, u - 1, first=not norms)
                    if prods and u == 2:
                        sums(g - 1, first=not norms)
                    if norms and u == 2:
                        variance2(g - 2)
                    if norms and u == 7:
                        wx(g - 2)

            pe.wait_ge(one_rows, 16)
            pe.wait_ge(stack_in[0], 16 * 4)
            pe.wait_ge(e_rows_in, 16 * 4)
            for step, first, end in ((center, 0, 2), (variance, 2, 3), (project_kq, 3, 5), (project_v, 5, 8)):
                step(PAIRS - 1)
                for u in range(first, end):
                    scores(0, u)
            pe.wait_ge(v_ready, G + CREDIT)
            pe.wait_ge(es_ready, G + CREDIT)
            pe.wait_ge(stack_in[1], 16 * 4)
            attend(1, 1, True, False)
            with pe.Fori(1, PAIRS) as i:
                pe.wait_ge(e_rows_in, 16 * 4 * i + 16 * 4)
                for par in range(2):
                    g = 2 * i + par
                    pe.wait_ge(stack_in[par], 16 * 4 * i + 16 * 4)
                    attend(g, par, True, True)
            center2(G - 2)
            for k in range(TT):
                products(G - 1, 1, k, False)
                if k == 1:
                    sums(G - 1, False)
                    variance2(G - 2)
            wx(G - 2)
            center2(G - 1)
            variance2(G - 1)
            wx(G - 1)

            pe.wait_ge(bn_c, 3)
            mm_(ps[:, 5, 0:2], c_("avg4"), mm, start=True, stop=True).then_inc(bn_pe, 1)
            pe.wait_ge(bn_c, 6)
            mm_(ps[:, 6, 0:P], c_("w"), diag[:, :], start=True, stop=True).then_inc(bn_pe, 1)
            pe.wait_ge(wsc_ready, 1)

            def steps(base, sweep, count):
                with pe.Fori(0, count // UNROLL) as i:
                    for k, bank in enumerate(BANKS):
                        s = UNROLL * i + k
                        if k == 0:
                            pe.wait_ge(start_ok, sweep + 1)
                        for h in range(2):
                            pe.wait_ge(y_ok[h], base + s + 1)
                            mm_(ps[:, 4 * h + bank, 0:HALF], wsc[:, :],
                                xl2[:, 4 * h:4 * h + 4, bass.ds(NC * s, NC)],
                                start=True, stop=False)
                        for h in range(2):
                            pe.wait_ge(y_ok[h], base + s + CREDIT)
                            mm_(ps[:, 4 * h + bank, 0:HALF], c_("vT"),
                                yb[:, bass.ds(s, 1), 4 * h:4 * h + 4, :].rearrange("p o g c -> p (o g c)"),
                                start=False, stop=True).then_inc(pre[h], 1)

            for sweep in range(2):
                steps(L * sweep, sweep, L)
            pe.wait_ge(cmp_c, 6)
            mm_(ps[0:1, 7, 0:1], okc, c_("ones")[:, 0:1], start=True, stop=True).then_inc(cmp_pe, 1)
            pe.wait_ge(flag_ok, 1)
            with pe.If(pe.value_load(flag[0:1, 0:1], min_val=0, max_val=1) != 0):
                with pe.Fori(0, NC - 1) as k:
                    steps(2 * L + L * k, k + 2, L)



def _blocks(a, n):
    r, c = a.shape
    m = np.zeros((n * r, n * c), a.dtype)
    for k in range(n):
        m[k * r:k * r + r, k * c:k * c + c] = a
    return m


def _constants(i):
    f = np.float32
    m = np.zeros((P, ALL_W), f)

    def put(name, a):
        o, w = COLUMNS[name]
        a = np.asarray(a)
        assert a.shape[1] == w, name
        m[0:a.shape[0], o:o + w] = a

    put("ident", np.eye(P, dtype=f))
    for name, a in (("al", i["L0_conv_A_learned"]), ("alT", i["L0_conv_A_learned"].T), ("intraT", i["L0_conv_A_intra"].T),
                    ("interT", i["L0_conv_A_inter"].T), ("flatT", i["L0_conv_A_flat"].T)):
        put(name, _blocks(a, TT))
    bn = np.ones((4, P, 3), f)
    bn[:, :, 0] = np.tile(i["L0_conv_bn_gc"], (1, NB))
    for j, name in enumerate(("bn_b1", "bn_b2", "bn_b3", "bn_b4")):
        bn[:, C * j:C * j + C, 1] = np.tile(i["L0_conv_" + name], (1, NB))
    for b in range(NB):
        for j, name in enumerate(("bn_t1", "bn_t2", "bn_p3")):
            bn[:, C * b + CB * j:C * b + CB * j + CB, 2] = i["L0_conv_" + name]
    for k, name in enumerate(("bn_g", "bn_b", "bn_m", "bn_v")):
        put(name, bn[k])
    keep = np.ones((P, 3), f)
    keep[np.arange(P) % C >= 3 * CB, 2] = 0
    put("keep", keep)
    put("pass", 1 - keep)
    r = np.arange(P)[:, None] % RB
    put("not_first", np.where(np.isin(r, (1, 2)), -1, 0).astype(f))
    put("third", np.where(r == 2, -1, 0).astype(f))
    put("gamma", np.tile(i["L1_ffn_gamma"], NB)[:, None])
    put("beta", np.tile(i["L1_ffn_beta"], NB)[:, None])
    put("eps", np.full((P, 1), LN_EPS, f))
    put("ones", np.ones((P, C), f))

    mix = np.zeros((2, NB, CH, NB, C), f)
    branch = np.zeros((P, BR, NB, CB), f)
    taps = np.zeros((len(OUTER), NB, CB, 2, NB, BR, CB), f)
    middle = np.zeros((BR, NB, CB, NB, BR, CB), f)
    for b in range(NB):
        mix[:, b, :, b] = i["L0_conv_Wgc"].T.reshape(2, CH, C)
        for j in range(BR):
            branch[C * b:C * b + C, j, b] = i[f"L0_conv_Wb{j + 1}"].T
        for j, name in enumerate(("Wt1", "Wt2")):
            w = i["L0_conv_" + name]
            for k, d in enumerate(OUTER):
                taps[k, b, :, j, b, j] = w[:, :, K // 2 + d].T
            middle[j, b, :, b, j] = w[:, :, K // 2].T
        for j in (2, 3):
            middle[j, b, :, b, j] = np.eye(CB, dtype=f)
    put("mix", mix.reshape(P, P))
    put("branch", branch.reshape(P, P))
    put("taps", taps.reshape(P, 2 * P))
    put("middle", middle.reshape(P, P))
    mean = np.full((C, C), 1 / C, f)
    put("mean", _blocks(mean, NB))
    put("center", _blocks(np.eye(C, dtype=f) - mean, NB))
    put("rotT", _blocks(i["L1_attn_rotation_params"].reshape(C, C).T, NB))
    put("entT", _blocks(i["L1_attn_entangle_params"].reshape(C, C).T, NB))
    put("wqT", _blocks(i["L1_attn_Wq"].T, NB))
    put("wkT", _blocks(i["L1_attn_Wk"].T, NB))
    put("wvT", _blocks(i["L1_attn_Wv"].T, NB))
    put("sel", _blocks(np.full((C, RB), -0.5, f), NB))
    put("wT", _blocks(i["L1_ffn_W"].T, NB))
    put("w", _blocks(i["L1_ffn_W"], NB))
    put("vT", _blocks(i["L1_ffn_V"].T, NB))
    put("avg4", np.tile(np.eye(C, dtype=f) / NB, (NB, NB)))
    return m


def kernel(**inputs):
    import concourse.bacc as bacc
    from concourse.bass_utils import run_bass_kernel_spmd

    i = {k: np.asarray(v) for k, v in inputs.items()}
    x = i["x"]
    by_token = x.reshape(G, NB, 2, CH, TT, MT).transpose(0, 5, 4, 2, 1, 3)
    arrays = {"x_tok": np.ascontiguousarray(by_token).reshape(G, MT, TT * P), "x": np.ascontiguousarray(x).reshape(G, P, N),
              "consts": _constants(i)}
    nc = bacc.Bacc("TRN2", target_bir_lowering=False, num_devices=1)
    args = [nc.dram_tensor(k, a.shape, F32, kind="ExternalInput").ap() for k, a in arrays.items()]
    out = nc.dram_tensor("out", (G, P, N), F32, kind="ExternalOutput").ap()
    build(nc, *args, out)
    got = run_bass_kernel_spmd(nc, [arrays], core_ids=[0]).results[0]["out"]
    return got.reshape(B, C, T, V)
```

```python
from contextlib import ExitStack

import numpy as np

import concourse.bass as bass
from concourse import mybir

F32 = mybir.dt.float32
BF16 = mybir.dt.bfloat16
I32 = mybir.dt.int32
ALU = mybir.AluOpType
ACT = mybir.ActivationFunctionType

B, C, T, V = 32, 32, 16, 25
N = T * V
NB = 4
G = B // NB
PAIRS = G // 2
P = NB * C
BR, CB, K = 4, C // 4, 5
CH = C // 2
TT, MT = 4, 100
OUTER = (-2, -1, 1, 2)
PAD = 4 * V
EPS = 1e-5
L = 10
NC = N // L
UNROLL = 5
BANKS = (0, 1, 2, 3, 1)
COLS = G * NC
HALF = COLS // 2
FULL = N // P
TAIL = N - FULL * P
TILES = NB * FULL + 1
UNITS = (TILES + 1) // 2
ADDS = NB * (FULL - 1)
PROB = TILES * N
RB = 8
TWO_ONES = float(np.frombuffer(np.uint32(0x3F803F80).tobytes(), np.float32)[0])
ARENA = 12600
MEET = (2.0 ** -18) ** 2

COLUMNS = {}


def _place(at, *entries):
    for name, width in entries:
        COLUMNS[name] = (at, width)
        at += width
    return at


LATE_W = _place(0, ("center", P), ("mean", P), ("wT", P), ("w", P), ("vT", P), ("avg4", P), ("tail_ones", P),
                ("mix", P), ("branch", P), ("taps", 2 * P), ("middle", P), ("rotT", P), ("wqT", P), ("entT", P),
                ("wkT", P), ("wvT", P), ("sel", C))
ALL_W = _place(LATE_W, ("al", MT), ("alT", MT), ("intraT", MT), ("interT", MT), ("flatT", MT), ("ident", P),
               ("bn_g", 3), ("bn_b", 3), ("bn_m", 3), ("bn_v", 3), ("keep", 3), ("pass", 3), ("not_first", 1),
               ("third", 1), ("gamma", 1), ("beta", 1), ("eps", 1), ("ones", C))


def build(nc, x_tok, x, consts, out):
    with ExitStack() as ctx:
        def sb(name, shape, dt=F32):
            return ctx.enter_context(nc.sbuf_tensor(name, shape, dt))

        def sem(name):
            return ctx.enter_context(nc.semaphore(name))

        cst = sb("cst", [P, ALL_W])

        def c_(name, rows=P):
            o, w = COLUMNS[name]
            return cst[0:rows, o:o + w]

        t0 = sb("t0", [P, G, N])
        vst = sb("vst", [P, G, P * FULL + C])
        ka, kb, qa, qb = ([sb(f"{name}{h}", [P, NB, N], BF16) for h in range(2)] for name in ("ka", "kb", "qa", "qb"))
        xl2 = sb("xl2", [P, G, N])
        yb = sb("yb", [P, L + 1, G, NC])
        ys, yd = (sb(name, [P, G, NC])[:, :, :] for name in ("ys", "yd"))
        outs = sb("outs", [P, G, N])
        arena = sb("arena", [P, ARENA])
        vb = sb("vb", [P, 2, 4 * P])
        prep = sb("prep", [P, 2 * P + 5 * MT])
        small = sb("small", [P, 64])
        stat = sb("stat", [P, G, 6])
        wsc = sb("wsc", [P, P])
        diag = sb("diag", [P, P])
        flag = sb("flag", [1, 1], I32)
        ps = ctx.enter_context(nc.psum_tensor("ps", [P, 8, 512], F32))
        sq = [sb(f"sq{h}", [P, N])[:, :] for h in range(2)]

        aq = prep[:, 0:2 * P].rearrange("p (k n) -> p k n", k=2)
        mlo = prep[0:MT, 2 * P:2 * P + 2 * MT].rearrange("p (k n) -> p k n", k=2)
        t2, ia, dd = (prep[0:MT, 2 * P + n * MT:2 * P + n * MT + MT] for n in (2, 3, 4))

        cut = [0]

        def piece(width, dt=F32):
            a = arena[:, cut[0]:cut[0] + width]
            cut[0] += width
            return a if dt == F32 else a.bitcast(dt)

        xks = piece(2 * TT * P).rearrange("p (g n) -> p g n", g=2)
        xk = [xks[:, h, :] for h in range(2)]
        y0 = [piece(N) for _ in range(2)]
        y4 = [piece(N) for _ in range(2)]
        zp = [piece(N + 2 * PAD) for _ in range(2)]
        tap_in = [[piece(N) for _ in range(2)] for _ in range(2)]
        mx, ts = y0, y4
        at_1 = max(cut[0], PROB)
        cut[0] = at_1
        rstd = [piece(N) for _ in range(2)]
        xl = [piece(N) for _ in range(2)]
        kp, qp = ([piece(3 * N // 2, BF16).rearrange("p (s n) -> p s n", n=N) for _ in range(2)]
                  for _ in range(2))
        rk = [piece(N) for _ in range(2)]
        rq = [piece(N) for _ in range(2)]
        es = piece(N)
        ep = piece(3 * N // 2, BF16).rearrange("p (s n) -> p s n", n=N)
        sqk, sqq = sq, rstd
        assert max(cut[0], at_1 + PROB + N) <= ARENA
        prob = [arena[:, o:o + PROB].rearrange("p (k n) -> p k n", k=TILES) for o in (0, at_1)]
        rden = arena[:, at_1 + PROB:at_1 + PROB + N]
        psum = sb("psum", [P, 2, NB, N])
        nrm, sq2 = sq
        rs2 = prep[:, 0:N]

        dka, dqa, dkb, dqb = (nc.dram_tensor(name, [G, P, n * N], BF16, kind="Internal").ap()
                              for name, n in (("dka", 4), ("dqa", 4), ("dkb", 2), ("dqb", 2)))
        de = nc.dram_tensor("de", [PAIRS, P, N], BF16, kind="Internal").ap()

        def col(n, w=1, rows=P):
            return small[0:rows, n:n + w]

        rowsum, dmax, dln, dcol = (col(n, 1, MT) for n in range(4))
        bn_ln, bn_r, bn_s, bn_ms, bn_h = (col(4 + 3 * n, 3) for n in range(5))
        bn_s2, bn_h2 = col(19, 3), col(22, 3)
        mv, mm, tot, m2, vv, lnv, rsv, scl, msc, shf, okc = (
            col(25, 2), col(27, 2), col(29, 2), *(col(n) for n in range(31, 39)))
        S_GC, S_Z, S_POST = 0, 1, 2
        K_AT, Q_AT = (0, 1, 2), (1, 2, 0)

        early_in, late_in, x_tok_in, x_in, one_rows, e_stored, out_done = (
            sem(n) for n in ("early_in", "late_in", "x_tok_in", "x_in", "one_rows",
                             "e_stored", "out_done"))
        kq_stored = [sem("kq_stored0"), sem("kq_stored1")]
        operands_in = [sem("operands_in0"), sem("operands_in1")]
        zeroed, abs_done, dve_c, act_c, pe_c, mlo_ready, prep_done = (
            sem(n) for n in ("zeroed", "abs_done", "dve_c", "act_c", "pe_c", "mlo_ready", "prep_done"))
        (v_mixed, y0_ready, mixed, y_ready, branched, zp_ready, mx_ready, u_ready, u_act, pooled, tapped, ts_ready,
         t0_ready) = (
            sem(n) for n in ("v_mixed", "y0_ready", "mixed", "y_ready", "branched", "zp_ready", "mx_ready",
                             "u_ready", "u_act", "pooled", "tapped", "ts_ready", "t0_ready"))
        (centered, sq_ready, var_done, ln_ready, rstd_ready, xl_ready, kq_done, k1_ready, q1_ready, rk_ready,
         rq_ready, seconds, parts_ready, v_done, v_ready, e_done, es_ready, e_step, e_ready) = (
            sem(n) for n in ("centered", "sq_ready", "var_done", "ln_ready", "rstd_ready", "xl_ready", "kq_done",
                             "k1_ready", "q1_ready", "rk_ready", "rq_ready", "seconds", "parts_ready", "v_done",
                             "v_ready", "e_done", "es_ready", "e_step", "e_ready"))
        (s_done, e1_done, p_ready, part_sum, psum_used, sums_done, vb_ready, pv_done, rden_ready, nrm_ready,
         t1_ready) = (
            sem(n) for n in ("s_done", "e1_done", "p_ready", "part_sum", "psum_used", "sums_done", "vb_ready",
                             "pv_done", "rden_ready", "nrm_ready", "t1_ready"))
        centered2, sq2_ready, var2_done, ln2_ready, rs2_ready, xl2_ready, wx_done, stat_ready = (
            sem(n) for n in ("centered2", "sq2_ready", "var2_done", "ln2_ready", "rs2_ready", "xl2_ready",
                             "wx_done", "stat_ready"))
        bn_c, bn_pe, bn_act, wsc_ready, start_ok, cmp_c, cmp_pe, flag_ok, added = (
            sem(n) for n in ("bn_c", "bn_pe", "bn_act", "wsc_ready", "start_ok", "cmp_c", "cmp_pe", "flag_ok",
                             "added"))
        pre = [sem("pre0"), sem("pre1")]
        y_ok = [sem("y_ok0"), sem("y_ok1")]
        CREDIT = 2
        CREDIT1 = 1
        CREDIT_DMA = 16
        OUT_G = 2

        def by_step(t, s):
            return t[:, :, :].rearrange("p g (c s) -> p s (g c)", s=L)[:, bass.ds(s, 1), :].rearrange("p o n -> p (o n)")

        NORM_BANKS = (6, 7)
        LAST_BANKS = {G - 3: NORM_BANKS, G - 2: (6, 1), G - 1: (2, 3)}

        def apart(eng):
            eng.wait_ge(early_in, 16)

        def tiles(u):
            return 2 * u, min(2 * u + 2, TILES)

        def slot(par, u):
            return (par * UNITS + u) % 2

        ACT_TAPS = (2, 3)

        def tap_input(par, j, k):
            o = PAD + V * OUTER[k] * (j + 1)
            return tap_in[par][j][C * k:C * k + C, :], zp[par][C * j:C * j + C, o:o + N]

        def at(t, g):
            return t[:, bass.ds(g, 1), :].rearrange("p o n -> p (o n)")

        block = ctx.enter_context(nc.Block())

        @block.sync
        def _(sp):
            sp.dma_start(cst[:, LATE_W:], consts[:, LATE_W:]).then_inc(early_in, 16)

            def load_tokens(i):
                sp.dma_start(xks[0:MT], x_tok[2 * i:2 * i + 2].rearrange("g p n -> p g n")).then_inc(x_tok_in, 16)

            def store(i):
                for par in range(2):
                    g = 2 * i + par
                    sp.wait_ge(parts_ready, 2 * g + 2)
                    kpp, qpp = kp[par], qp[par]
                    for scratch, lo, hi, part in (
                            (dka, 0, 2, kpp[:, 0:1].to_broadcast([P, 2, N])),
                            (dka, 2, 4, kpp[:, 1:2].to_broadcast([P, 2, N])),
                            (dqa, 0, 2, qpp[:, 1:3]), (dqa, 2, 4, qpp[:, 1:3]),
                            (dkb, 0, 2, kpp[:, 0:3:2]),
                            (dqb, 0, 2, qpp[:, 0:2])):
                        sp.dma_start(scratch[bass.ds(g, 1), :, N * lo:N * hi].rearrange("o p (s n) -> (o p) s n", n=N),
                                     part).then_inc(kq_stored[par], 16)
                sp.wait_ge(e_ready, i + 1 + CREDIT1)
                sp.dma_start(de[bass.ds(i, 1)].rearrange("o p n -> p (o n)"), ep[:, 2, :]).then_inc(e_stored, 16)

            def load_operands(i, par):
                g = 2 * i + par
                sp.wait_ge(kq_stored[par], 96 * i + 96 + CREDIT_DMA)
                sp.wait_ge(e_stored, 16 * i + 16 + CREDIT_DMA)
                for dst, scratch, n in ((ka, dka, 4), (qa, dqa, 4), (kb, dkb, 2), (qb, dqb, 2)):
                    sp.dma_start(dst[par][0:n * C, :, :], scratch[bass.ds(g, 1)].rearrange(
                        "o (b c) (s n) -> (c s) (o b) n", b=NB, n=N)).then_inc(operands_in[par], 16)
                rows = de[bass.ds(i, 1)].rearrange("o (g h b r) n -> g h r (o b) n", g=2, h=2, b=NB)
                for h, (dst, row) in enumerate(((kb, 2 * C), (qb, 2 * C + 3))):
                    sp.dma_start(dst[par][row:row + 3, :, :], rows[par, h, 0:3]).then_inc(operands_in[par], 16)

            load_tokens(0)
            sp.dma_start(t0[:, :, :], x.rearrange("g p n -> p g n")).then_inc(x_in, 16)
            for s in (*kq_stored, e_stored):
                sp.sem_inc(s, CREDIT_DMA)
            sp.wait_ge(zeroed, 8)
            for h in range(2):
                sp.dma_start(kb[h][67:70, :, :], qb[h][64:67, :, :]).then_inc(one_rows, 16)
            sp.wait_ge(one_rows, 32)
            for i in range(PAIRS - 1):
                sp.wait_ge(v_mixed, 2 * i + 2)
                load_tokens(i + 1)
            store(0)
            for par in range(2):
                load_operands(0, par)
            with sp.Fori(1, PAIRS) as i:
                store(i)
            with sp.Fori(1, PAIRS) as i:
                for par in range(2):
                    sp.wait_ge(s_done, UNITS * (2 * i + par - 1))
                    load_operands(i, par)
            def store_output(sums):
                sp.wait_ge(added, L * sums)
                for g in range(0, G, OUT_G):
                    sp.dma_start(out[g:g + OUT_G].rearrange("g p n -> p g n"),
                                 outs[:, g:g + OUT_G, :]).then_inc(out_done, 16)
                sp.wait_ge(out_done, 16 * (G // OUT_G) * sums)

            store_output(1)
            sp.wait_ge(flag_ok, 1)
            with sp.If(sp.value_load(flag[0:1, 0:1], min_val=0, max_val=1) != 0):
                store_output(2)

        @block.gpsimd
        def _(pool):
            fills = [(zp[h][:, o:o + PAD], 0.0) for h in range(2) for o in (0, PAD + N)]
            fills += [(t[h][64:96, :, :].rearrange("p b n -> p (b n)").bitcast(F32), v)
                      for t, v in ((kb, 0.0), (qb, TWO_ONES)) for h in range(2)]
            for n, (t, v) in enumerate(fills):
                if n:
                    pool.wait_ge(zeroed, n)
                nc.gpsimd.memset(t, v).then_inc(zeroed, 1)
            pool.wait_ge(zeroed, len(fills))
            pool.wait_ge(early_in, 16)

            def square_parts(i):
                a, b, f = (ep[:, s, :] for s in range(3))
                pool.wait_ge(es_ready, 2 * i + 2 + CREDIT)
                pool.wait_ge(e_stored, 16 * i + CREDIT_DMA)
                nc.gpsimd.tensor_tensor(a, es, c_("not_first").to_broadcast([P, N]), ALU.mult).then_inc(e_step, 1)
                pool.wait_ge(e_step, 3 * i + 1)
                nc.gpsimd.tensor_tensor(es, es, a, ALU.add).then_inc(e_step, 1)
                pool.wait_ge(e_step, 3 * i + 2)
                nc.gpsimd.tensor_tensor(b, es, c_("third").to_broadcast([P, N]), ALU.mult).then_inc(e_step, 1)
                pool.wait_ge(e_step, 3 * i + 3)
                nc.gpsimd.tensor_tensor(f, es, b, ALU.add).then_inc(e_ready, 1)

            def values(g, par):
                nc.gpsimd.tensor_copy(vb[:, par, 0:P * FULL],
                                      vst[:, bass.ds(g, 1), 0:P * FULL].rearrange("p o n -> p (o n)"))
                nc.gpsimd.tensor_tensor(
                    vb[:, par, P * FULL:].rearrange("p (b c) -> p b c", b=NB),
                    vst[:, bass.ds(g, 1), P * FULL:].to_broadcast([P, NB, C]),
                    c_("tail_ones").rearrange("p (b c) -> p b c", b=NB), ALU.mult).then_inc(vb_ready, 1)

            square_parts(0)
            for par in range(2):
                values(par, par)
            with pool.Fori(1, PAIRS) as i:
                square_parts(i)
            with pool.Fori(0, PAIRS - 1) as i:
                for par in range(2):
                    pool.wait_ge(pv_done, 2 * i + par + 1)
                    apart(pool)
                    values(2 * i + 2 + par, par)

        @block.scalar
        def _(act):
            act.dma_start(cst[:, 0:LATE_W], consts[:, 0:LATE_W]).then_inc(late_in, 16)
            nc.scalar.preload_act_table_set("natural_log_exp_and_others")
            act.wait_ge(early_in, 16)
            nc.scalar.activation(dd, c_("al", MT), ACT.Abs, accum_out=rowsum)
            nc.scalar.activation(t2, c_("alT", MT), ACT.Abs).then_inc(abs_done, 1)
            nc.scalar.activation(bn_ln, c_("bn_v"), ACT.Ln, bias=c_("eps")).then_inc(act_c, 1)
            act.wait_ge(act_c, 1)
            nc.scalar.activation(bn_r, bn_ln, ACT.Exp, scale=-0.5).then_inc(act_c, 1)
            act.wait_ge(dve_c, 1)
            nc.scalar.activation(dln, dmax, ACT.Ln).then_inc(act_c, 1)
            act.wait_ge(act_c, 3)
            nc.scalar.activation(dcol, dln, ACT.Exp, scale=-0.5).then_inc(act_c, 1)
            act.wait_ge(prep_done, 1)

            def y_relu(i):
                for par in range(2):
                    act.wait_ge(mixed, 2 * i + par + 1)
                    nc.scalar.activation(y4[par], ps[:, 2 * par + 1, 0:N], ACT.Relu, bias=bn_h2[:, S_GC:S_GC + 1],
                                         scale=bn_s2[:, S_GC:S_GC + 1]).then_inc(y_ready, 1)

            def branches(i):
                for par in range(2):
                    act.wait_ge(branched, 2 * i + par + 1)
                    for lo, hi, f in ((0, 96, ACT.Relu), (96, P, ACT.Identity)):
                        last = nc.scalar.activation(zp[par][lo:hi, PAD:PAD + N], ps[lo:hi, 2 * par, 0:N], f,
                                                    bias=bn_h2[lo:hi, S_Z:S_Z + 1], scale=bn_s2[lo:hi, S_Z:S_Z + 1])
                    last.then_inc(zp_ready, 1)
                for par in range(2):
                    act.wait_ge(zp_ready, 2 * i + par + 1)
                    for k in ACT_TAPS:
                        last = nc.scalar.copy(*tap_input(par, 1, k))
                    last.then_inc(u_act, 1)

            def t_relu(i):
                for par in range(2):
                    g = 2 * i + par
                    act.wait_ge(ts_ready, g + 1)
                    nc.scalar.activation(at(t0, g), ts[par], ACT.Relu,
                                         bias=bn_h2[:, S_POST:S_POST + 1]).then_inc(t0_ready, 1)

            def squares(i):
                for par in range(2):
                    act.wait_ge(centered, 2 * i + par + 1)
                    nc.scalar.activation(sq[par], ps[:, 4 + 2 * par, 0:N], ACT.Square).then_inc(sq_ready, 1)

            def inverse_roots(i):
                for par in range(2):
                    act.wait_ge(var_done, 2 * i + par + 1)
                    nc.scalar.activation(rstd[par], ps[:, 5 + 2 * par, 0:N], ACT.Ln,
                                         bias=c_("eps")).then_inc(ln_ready, 1)
                for par in range(2):
                    act.wait_ge(ln_ready, 2 * i + par + 1)
                    nc.scalar.activation(rstd[par], rstd[par], ACT.Exp, scale=-0.5).then_inc(rstd_ready, 1)

            def kq_firsts(i):
                for par in range(2):
                    g = 2 * i + par
                    act.wait_ge(kq_done, g + 1)
                    act.wait_ge(kq_stored[par], 96 * i + CREDIT_DMA)
                    for parts, slot, s, n, ready in ((kp, K_AT[0], sqk, 4, k1_ready), (qp, Q_AT[0], sqq, 5, q1_ready)):
                        nc.scalar.copy(parts[par][:, slot, :], ps[:, n + 2 * par, 0:N])
                        nc.scalar.activation(s[par], ps[:, n + 2 * par, 0:N], ACT.Square).then_inc(ready, 1)

            def v_and_squares(i):
                for par in range(2):
                    g = 2 * i + par
                    act.wait_ge(v_done, g + 1)
                    nc.scalar.copy(at(vst, g), ps[:, 4 + 2 * par, 0:P * FULL + C]).then_inc(v_ready, 1)
                    act.wait_ge(e_done, g + 1)
                    act.wait_ge(e_ready, i + 1)
                    lo, hi = 2 * C * par, 2 * C * (par + 1)
                    nc.scalar.copy(es[lo:hi], ps[lo:hi, 5 + 2 * par, 0:N]).then_inc(es_ready, 1)

            y_relu(0)
            branches(0)
            t_relu(0)
            with act.Fori(0, PAIRS - 1) as i:
                squares(i)
                y_relu(i + 1)
                inverse_roots(i)
                branches(i + 1)
                kq_firsts(i)
                t_relu(i + 1)
                v_and_squares(i)

            def inner(g, par, u):
                act.wait_ge(s_done, UNITS * g + u + 1)
                lo, hi = tiles(u)
                o = 2 * slot(par, u)
                nc.scalar.activation(prob[par][:, lo:hi, :], ps[:, o:o + hi - lo, 0:N], ACT.Exp,
                                     scale=2.0).then_inc(e1_done, 1)

            def outer(g, par, u):
                act.wait_ge(e1_done, UNITS * g + u + 1)
                lo, hi = tiles(u)
                p = prob[par][:, lo:hi, :]
                nc.scalar.activation(p, p, ACT.Exp).then_inc(p_ready, 1)

            def norm2(g, step, banks=NORM_BANKS):
                if step == 0:
                    act.wait_ge(centered2, g + 1)
                    nc.scalar.activation(sq2, ps[:, banks[0], 0:N], ACT.Square).then_inc(sq2_ready, 1)
                elif step == 1:
                    act.wait_ge(var2_done, g + 1)
                    if banks[0] != NORM_BANKS[0]:
                        act.wait_ge(xl2_ready, g + CREDIT1)
                    nc.scalar.activation(rs2, ps[:, banks[1], 0:N], ACT.Ln, bias=c_("eps")).then_inc(ln2_ready, 1)
                else:
                    act.wait_ge(ln2_ready, g + 1)
                    nc.scalar.activation(rs2, rs2, ACT.Exp, scale=-0.5).then_inc(rs2_ready, 1)

            def weights(g, par):
                since = g if isinstance(g, int) else G
                if since > 1:
                    act.wait_ge(pv_done, g - 1)
                for u in range(UNITS):
                    if since == 1 and u == 2:
                        for h in range(2):
                            act.wait_ge(kq_stored[h], 96 * PAIRS + CREDIT_DMA)
                    inner(g, par, u)
                    if u:
                        outer(g, par, u - 1)
                    elif since > 0:
                        outer(g - 1, 1 - par, UNITS - 1)
                    if u in (0, 1) and since > 2:
                        norm2(g - 3, u + 1)
                    if u == 4 and since > 1:
                        norm2(g - 2, 0)

            for step, first, end in ((squares, 0, 2), (inverse_roots, 2, 3), (kq_firsts, 3, 5),
                                     (v_and_squares, 5, UNITS)):
                step(PAIRS - 1)
                for u in range(first, end):
                    inner(0, 0, u)
                    if u:
                        outer(0, 0, u - 1)
            for g in range(1, 4):
                weights(g, g % 2)
            with act.Fori(2, PAIRS) as i:
                for par in range(2):
                    weights(2 * i + par, par)
            outer(G - 1, 1, UNITS - 1)
            for step in range(1, 3):
                norm2(G - 3, step)
            for g in (G - 2, G - 1):
                for step in range(3):
                    norm2(g, step, LAST_BANKS[g])
            act.wait_ge(bn_c, 4)
            nc.scalar.activation(lnv, vv, ACT.Ln, bias=c_("eps")).then_inc(bn_act, 1)
            act.wait_ge(bn_act, 1)
            nc.scalar.activation(rsv, lnv, ACT.Exp, scale=-0.5).then_inc(bn_act, 1)

            nc.scalar.preload_act_table_set("sigmoid_and_others")
            act.wait_ge(wsc_ready, 1)
            act.wait_ge(bn_c, 8)

            def steps(base, count):
                with act.Fori(0, count // UNROLL) as i:
                    for k, bank in enumerate(BANKS):
                        s = UNROLL * i + k
                        for h in range(2):
                            act.wait_ge(pre[h], base + s + 1)
                            nc.scalar.activation(
                                yb[:, bass.ds(s + 1, 1), 4 * h:4 * h + 4, :].rearrange("p o g c -> p (o g c)"),
                                ps[:, 4 * h + bank, 0:HALF], ACT.Sigmoid, bias=shf).then_inc(y_ok[h], 1)

            steps(0, L)
            act.wait_ge(cmp_c, 3)
            steps(L, L)
            act.wait_ge(flag_ok, 1)
            with act.If(act.value_load(flag[0:1, 0:1], min_val=0, max_val=1) != 0):
                with act.Fori(0, NC - 1) as k:
                    steps(2 * L + L * k, L)

        @block.vector
        def _(dve):
            count = [0]

            def link(ins, s=dve_c, c=count):
                c[0] += 1
                ins.then_inc(s, 1)
                dve.wait_ge(s, c[0])

            dve.wait_ge(early_in, 16)
            dve.wait_ge(abs_done, 1)
            link(nc.vector.tensor_scalar(dmax, rowsum, 1e-6, None, ALU.max))
            dve.wait_ge(act_c, 4)
            link(nc.vector.tensor_scalar(dd, c_("ident", MT)[:, 0:MT], dcol, None, ALU.mult))
            dve.wait_ge(pe_c, 1)
            link(nc.vector.scalar_tensor_tensor(out=ia, in0=ps[0:MT, 2, 0:MT], scalar=dcol,
                                                in1=c_("ident", MT)[:, 0:MT], op0=ALU.mult, op1=ALU.add))
            dve.wait_ge(pe_c, 3)
            nc.vector.tensor_copy(mlo[:, 0, :], ps[0:MT, 2, 0:MT])
            link(nc.vector.tensor_copy(t2, ps[0:MT, 3, 0:MT]))
            dve.wait_ge(pe_c, 4)
            nc.vector.tensor_copy(mlo[:, 1, :], ps[0:MT, 0, 0:MT]).then_inc(mlo_ready, 1)
            link(nc.vector.tensor_tensor(bn_s, bn_r, c_("bn_g"), ALU.mult))
            link(nc.vector.tensor_tensor(bn_ms, bn_s, c_("bn_m"), ALU.mult))
            link(nc.vector.tensor_tensor(bn_h, c_("bn_b"), bn_ms, ALU.subtract))
            link(nc.vector.tensor_tensor(bn_h2, bn_h, c_("keep"), ALU.mult))
            link(nc.vector.tensor_tensor(bn_s, bn_s, c_("keep"), ALU.mult))
            link(nc.vector.tensor_tensor(bn_s2, bn_s, c_("pass"), ALU.add))
            dve.wait_ge(pe_c, 6)
            nc.vector.tensor_copy(aq[:, 0, :], ps[:, 6, 0:P])
            nc.vector.tensor_copy(aq[:, 1, :], ps[:, 7, 0:P]).then_inc(prep_done, 1)
            dve.wait_ge(zeroed, 4)

            def y_copy(i):
                for par in range(2):
                    dve.wait_ge(v_mixed, 2 * i + par + 1)
                    nc.vector.tensor_copy(y0[par], ps[:, 2 * par, 0:N]).then_inc(y0_ready, 1)

            def tap_inputs(i):
                for par in range(2):
                    g = 2 * i + par
                    z = zp[par]
                    dve.wait_ge(zp_ready, g + 1)
                    nc.vector.tensor_tensor(mx[par][64:96, :], z[64:96, PAD - V:PAD - V + N],
                                            z[64:96, PAD + V:PAD + V + N], ALU.max).then_inc(mx_ready, 1)
                    for j in range(2):
                        for k in range(len(OUTER)):
                            if j == 0 or k not in ACT_TAPS:
                                last = nc.vector.tensor_copy(*tap_input(par, j, k))
                        last.then_inc(u_ready, 1)
                    dve.wait_ge(mx_ready, g + 1)
                    mid = z[64:96, PAD:PAD + N]
                    nc.vector.tensor_tensor(mid, mid, mx[par][64:96, :], ALU.max).then_inc(pooled, 1)

            def add_x(i):
                for par in range(2):
                    dve.wait_ge(tapped, 2 * i + par + 1)
                    nc.vector.scalar_tensor_tensor(out=ts[par], in0=ps[:, 2 * par + 1, 0:N],
                                                   scalar=bn_s2[:, S_POST:S_POST + 1], in1=at(t0, 2 * i + par),
                                                   op0=ALU.mult, op1=ALU.add).then_inc(ts_ready, 1)

            def norm(i):
                for par in range(2):
                    g = 2 * i + par
                    dve.wait_ge(rstd_ready, g + 1)
                    nc.vector.tensor_tensor(xl[par], ps[:, 4 + 2 * par, 0:N], rstd[par],
                                            ALU.mult).then_inc(xl_ready, 1)

            def rests(i):
                for par in range(2):
                    g = 2 * i + par
                    dve.wait_ge(k1_ready, g + 1)
                    nc.vector.tensor_tensor(rk[par], ps[:, 4 + 2 * par, 0:N], kp[par][:, K_AT[0], :],
                                            ALU.subtract).then_inc(rk_ready, 1)
                    dve.wait_ge(q1_ready, g + 1)
                    nc.vector.tensor_tensor(rq[par], ps[:, 5 + 2 * par, 0:N], qp[par][:, Q_AT[0], :],
                                            ALU.subtract).then_inc(rq_ready, 1)

            def parts(i):
                for par in range(2):
                    g = 2 * i + par
                    for n, (r, p, slots) in enumerate(((rk, kp, K_AT), (rq, qp, Q_AT))):
                        dve.wait_ge((rk_ready, rq_ready)[n], g + 1)
                        nc.vector.tensor_copy(p[par][:, slots[1], :], r[par]).then_inc(seconds, 1)
                    for n, (r, p, slots) in enumerate(((rk, kp, K_AT), (rq, qp, Q_AT))):
                        dve.wait_ge(seconds, 2 * g + n + 1)
                        nc.vector.tensor_tensor(p[par][:, slots[2], :], r[par], p[par][:, slots[1], :],
                                                ALU.subtract).then_inc(parts_ready, 1)

            dve.wait_ge(x_in, 16)
            y_copy(0)
            tap_inputs(0)
            add_x(0)
            with dve.Fori(0, PAIRS - 1) as i:
                y_copy(i + 1)
                norm(i)
                tap_inputs(i + 1)
                rests(i)
                add_x(i + 1)
                parts(i)
            norm(PAIRS - 1)
            rests(PAIRS - 1)
            parts(PAIRS - 1)

            def add_tiles(g, par, u):
                dve.wait_ge(p_ready, UNITS * g + u + 1)
                for t in range(*tiles(u)):
                    b, k = divmod(t, FULL)
                    if b == NB or k == 0:
                        continue
                    dst = psum[:, par, b, :]
                    if k == 1:
                        a = prob[par][:, t - 1, :]
                    else:
                        a = dst
                        dve.wait_ge(part_sum, ADDS * g + (FULL - 1) * b + k - 1)
                    nc.vector.tensor_tensor(dst, a, prob[par][:, t, :], ALU.add).then_inc(part_sum, 1)

            def reciprocals(g, first=False):
                dve.wait_ge(sums_done, g + 1)
                if first:
                    for h in range(2):
                        dve.wait_ge(kq_stored[h], 96 * PAIRS + CREDIT_DMA)
                else:
                    dve.wait_ge(nrm_ready, g)
                nc.vector.reciprocal(rden, ps[:, 5, 0:N]).then_inc(rden_ready, 1)

            def quotient(g, first=False):
                dve.wait_ge(pv_done, g + 1)
                dve.wait_ge(rden_ready, g + 1)
                if not first:
                    dve.wait_ge(t1_ready, g)
                nc.vector.tensor_tensor(nrm, ps[:, 4, 0:N], rden, ALU.mult).then_inc(nrm_ready, 1)

            def residual(g):
                dve.wait_ge(nrm_ready, g + 1)
                nc.vector.tensor_tensor(at(t0, g), at(t0, g), nrm, ALU.add).then_inc(t1_ready, 1)

            def norm2(g, banks=NORM_BANKS):
                dve.wait_ge(rs2_ready, g + 1)
                nc.vector.tensor_tensor(at(xl2, g).rearrange("p (s c) -> p s c", s=L),
                                        ps[:, banks[0], 0:N].rearrange("p (c s) -> p s c", s=L),
                                        rs2.rearrange("p (c s) -> p s c", s=L), ALU.mult).then_inc(xl2_ready, 1)

            def stats(g, banks=NORM_BANKS):
                dve.wait_ge(wx_done, g + 1)
                nc.vector.bn_stats(at(stat, g), ps[:, banks[1], 0:N]).then_inc(stat_ready, 1)

            def attend(g, par):
                since = g if isinstance(g, int) else G
                if since > 1:
                    dve.wait_ge(psum_used, g - 1)
                for u in range(UNITS - 1):
                    add_tiles(g, par, u)
                    if since > 2 and u == 0:
                        norm2(g - 3)
                    if since > 0 and u == 2:
                        reciprocals(g - 1, first=since == 1)
                    if since > 2 and u == 2:
                        stats(g - 3)
                    if since > 0 and u == 4:
                        quotient(g - 1, first=since == 1)
                        residual(g - 1)

            for g in range(4):
                attend(g, g % 2)
            with dve.Fori(2, PAIRS) as i:
                for par in range(2):
                    attend(2 * i + par, par)
            norm2(G - 3)
            stats(G - 3)
            reciprocals(G - 1)
            norm2(G - 2, LAST_BANKS[G - 2])
            quotient(G - 1)
            residual(G - 1)
            stats(G - 2, LAST_BANKS[G - 2])
            norm2(G - 1, LAST_BANKS[G - 1])
            stats(G - 1, LAST_BANKS[G - 1])

            bc = [0]

            def blink(ins):
                link(ins, bn_c, bc)

            dve.wait_ge(stat_ready, G + CREDIT1)
            blink(nc.vector.bn_aggr(mv, stat[:, :, :].rearrange("p g s -> p (g s)")))
            blink(nc.vector.tensor_tensor(m2, mv[:, 0:1], mv[:, 0:1], ALU.mult))
            nc.vector.tensor_copy(mm[:, 0:1], mv[:, 0:1])
            blink(nc.vector.tensor_tensor(mm[:, 1:2], mv[:, 1:2], m2, ALU.add))
            dve.wait_ge(bn_pe, 1)
            nc.vector.tensor_copy(tot, ps[:, 5, 0:2]).then_inc(cmp_c, 1)
            dve.wait_ge(cmp_c, 1)
            nc.vector.tensor_tensor(m2, tot[:, 0:1], tot[:, 0:1], ALU.mult).then_inc(cmp_c, 1)
            dve.wait_ge(cmp_c, 2)
            blink(nc.vector.tensor_tensor(vv, tot[:, 1:2], m2, ALU.subtract))
            dve.wait_ge(bn_act, 2)
            blink(nc.vector.tensor_tensor(scl, rsv, c_("gamma"), ALU.mult))
            blink(nc.vector.tensor_scalar(diag[:, :], c_("ident"), scl, None, ALU.mult))
            blink(nc.vector.tensor_tensor(msc, tot[:, 0:1], scl, ALU.mult))
            blink(nc.vector.tensor_tensor(shf, c_("beta"), msc, ALU.subtract))
            nc.vector.memset(yb[:, 0, :, :], 0.0).then_inc(start_ok, 1)
            dve.wait_ge(bn_pe, 2)
            nc.vector.tensor_copy(wsc[:, :], ps[:, 6, 0:P]).then_inc(wsc_ready, 1)

            def chain(base):
                for h in range(2):
                    dve.wait_ge(y_ok[h], base + CREDIT)
                nc.vector.tensor_copy(yb[:, 0, :, 1:NC], yb[:, L, :, 0:NC - 1]).then_inc(start_ok, 1)

            chain(L)
            nc.vector.tensor_copy(ys, yb[:, L, :, :]).then_inc(cmp_c, 1)

            def add_residual():
                with dve.Fori(0, L // UNROLL) as i:
                    for k in range(UNROLL):
                        j = UNROLL * i + k
                        for h in range(2):
                            dve.wait_ge(y_ok[h], L + j + 1 + CREDIT)
                        nc.vector.tensor_tensor(by_step(outs, j), by_step(t0, j),
                                                yb[:, bass.ds(j + 1, 1), :, :].rearrange("p o g c -> p (o g c)"),
                                                ALU.add).then_inc(added, 1)

            add_residual()
            dve.wait_ge(cmp_c, 3)
            nc.vector.tensor_tensor(yd, yb[:, L, :, :], ys, ALU.subtract).then_inc(cmp_c, 1)
            dve.wait_ge(cmp_c, 4)
            nc.vector.tensor_tensor(ys, yd, yd, ALU.mult).then_inc(cmp_c, 1)
            dve.wait_ge(cmp_c, 5)
            nc.vector.tensor_scalar(yd, ys, MEET, None, ALU.is_le, ALU.add, accum_out=okc).then_inc(cmp_c, 1)
            dve.wait_ge(cmp_pe, 1)
            nc.vector.tensor_scalar(flag[0:1, 0:1], ps[0:1, 7, 0:1], float(P * COLS), None,
                                    ALU.not_equal).then_inc(flag_ok, 1)
            dve.wait_ge(flag_ok, 1)
            with dve.If(dve.value_load(flag[0:1, 0:1], min_val=0, max_val=1) != 0):
                with dve.Fori(0, NC - 1) as k:
                    chain(2 * L + L * k)
                for h in range(2):
                    dve.wait_ge(y_ok[h], 2 * L + L * (NC - 1) + CREDIT)
                dve.wait_ge(out_done, 16 * (G // OUT_G))
                add_residual()

        @block.tensor
        def _(pe):
            mm_ = nc.tensor.matmul
            for s in (v_ready, es_ready, *y_ok):
                pe.sem_inc(s, CREDIT)
            for s in (e_ready, xl2_ready, stat_ready):
                pe.sem_inc(s, CREDIT1)
            pe.wait_ge(dve_c, 2)
            mm_(ps[0:MT, 2, 0:MT], t2, dd, start=True, stop=True).then_inc(pe_c, 1)
            pe.wait_ge(dve_c, 3)
            mm_(ps[0:MT, 2, 0:MT], c_("intraT", MT), ia, start=True, stop=True).then_inc(pe_c, 1)
            mm_(ps[0:MT, 3, 0:MT], c_("interT", MT), ia, start=True, stop=True).then_inc(pe_c, 1)
            pe.wait_ge(dve_c, 4)
            mm_(ps[0:MT, 0, 0:MT], c_("flatT", MT), t2, start=True, stop=True).then_inc(pe_c, 1)
            pe.wait_ge(late_in, 16)
            mm_(ps[:, 6, 0:P], c_("rotT"), c_("wqT"), start=True, stop=True).then_inc(pe_c, 1)
            mm_(ps[:, 7, 0:P], c_("entT"), c_("wkT"), start=True, stop=True).then_inc(pe_c, 1)
            pe.wait_ge(mlo_ready, 1)

            def mix_v(i):
                pe.wait_ge(x_tok_in, 16 * i + 16)
                for par in range(2):
                    if not isinstance(i, int):
                        pe.wait_ge(zp_ready, 2 * i + par - 1)
                    for tt in range(TT):
                        for h in range(2):
                            o = P * tt + NB * CH * h
                            last = mm_(ps[NB * CH * h:NB * CH * (h + 1), 2 * par, MT * tt:MT * tt + MT],
                                       xk[par][0:MT, o:o + NB * CH], mlo[:, h, :], start=True, stop=True,
                                       skip_group_check=True)
                    last.then_inc(v_mixed, 1)

            def mix_c(i):
                for par in range(2):
                    pe.wait_ge(y0_ready, 2 * i + par + 1)
                    if not isinstance(i, int):
                        pe.wait_ge(ts_ready, 2 * i + par - 1)
                    mm_(ps[:, 2 * par + 1, 0:N], c_("mix"), y0[par], start=True, stop=True).then_inc(mixed, 1)

            def branches(i):
                for par in range(2):
                    pe.wait_ge(y_ready, 2 * i + par + 1)
                    mm_(ps[:, 2 * par, 0:N], c_("branch"), y4[par], start=True, stop=True).then_inc(branched, 1)

            def taps(i):
                for par in range(2):
                    o = COLUMNS["taps"][0]
                    for j in range(2):
                        pe.wait_ge(u_ready, 2 * (2 * i + par) + j + 1)
                        if j:
                            pe.wait_ge(u_act, 2 * i + par + 1)
                        mm_(ps[:, 2 * par + 1, 0:N], cst[:, o + P * j:o + P * j + P], tap_in[par][j],
                            start=(j == 0), stop=False)
                    pe.wait_ge(pooled, 2 * i + par + 1)
                    mm_(ps[:, 2 * par + 1, 0:N], c_("middle"), zp[par][:, PAD:PAD + N],
                        start=False, stop=True).then_inc(tapped, 1)

            def center(i):
                for par in range(2):
                    g = 2 * i + par
                    pe.wait_ge(t0_ready, g + 1)
                    pe.wait_ge(v_ready, g + 1)
                    mm_(ps[:, 4 + 2 * par, 0:N], c_("center"), at(t0, g), start=True, stop=True).then_inc(centered, 1)

            def variance(i):
                for par in range(2):
                    g = 2 * i + par
                    pe.wait_ge(sq_ready, g + 1)
                    pe.wait_ge(es_ready, g + 1)
                    mm_(ps[:, 5 + 2 * par, 0:N], c_("mean"), sq[par], start=True, stop=True).then_inc(var_done, 1)

            def project_kq(i):
                for par in range(2):
                    pe.wait_ge(xl_ready, 2 * i + par + 1)
                    mm_(ps[:, 4 + 2 * par, 0:N], aq[:, 1, :], xl[par], start=True, stop=True)
                    mm_(ps[:, 5 + 2 * par, 0:N], aq[:, 0, :], xl[par], start=True, stop=True).then_inc(kq_done, 1)

            def project_v(i):
                for par in range(2):
                    g = 2 * i + par
                    pe.wait_ge(rk_ready, g + 1)
                    for k in range(FULL):
                        mm_(ps[:, 4 + 2 * par, P * k:P * k + P], xl[par][:, P * k:P * k + P], c_("wvT"),
                            start=True, stop=True, skip_group_check=True)
                    for b in range(NB):
                        last = mm_(ps[C * b:C * b + C, 4 + 2 * par, P * FULL:P * FULL + C], xl[par][:, N - C:N],
                                   c_("wvT")[:, C * b:C * b + C], start=True, stop=True, skip_group_check=True)
                    last.then_inc(v_done, 1)
                    pe.wait_ge(rq_ready, g + 1)
                    for n, s in enumerate((sqk, sqq)):
                        o = 2 * C * par + C * n
                        last = mm_(ps[o:o + C, 5 + 2 * par, 0:N], c_("sel"), s[par], start=True, stop=True,
                                   skip_group_check=True)
                    last.then_inc(e_done, 1)

            mix_v(0)
            pe.wait_ge(prep_done, 1)
            mix_c(0)
            branches(0)
            taps(0)
            with pe.Fori(0, PAIRS - 1) as i:
                mix_v(i + 1)
                center(i)
                mix_c(i + 1)
                variance(i)
                branches(i + 1)
                project_kq(i)
                taps(i + 1)
                project_v(i)

            def scores(g, par, u):
                if u >= 2 or not isinstance(g, int) or g > 0:
                    pe.wait_ge(e1_done, UNITS * g + u - 1)
                for t in range(*tiles(u)):
                    bank = 2 * slot(par, u) + t % 2
                    if t < TILES - 1:
                        blocks = [(0, t // FULL, P * (t % FULL), P)]
                    else:
                        blocks = [(C * b, b, N - C, C) for b in range(NB)]
                    for row, b, o, keys in blocks:
                        for kk, qq, rows, first in ((ka, qa, P, True), (kb, qb, 96, False)):
                            last = mm_(ps[row:row + keys, bank, 0:N],
                                       kk[par][0:rows, b, o:o + keys], qq[par][0:rows, b, :],
                                       start=first, stop=not first, skip_group_check=True)
                last.then_inc(s_done, 1)

            def sums(g, par, first):
                pe.wait_ge(part_sum, ADDS * (g + 1))
                if not first:
                    pe.wait_ge(rden_ready, g)
                for b in range(NB):
                    last = mm_(ps[C * b:C * b + C, 5, 0:N], c_("ones"), psum[:, par, b, :], start=True, stop=False,
                               skip_group_check=True)
                last.then_inc(psum_used, 1)

            def tail_sums(g, par):
                pe.wait_ge(p_ready, UNITS * (g + 1))
                mm_(ps[:, 5, 0:N], c_("tail_ones"), prob[par][:, TILES - 1, :], start=False, stop=True,
                    skip_group_check=True).then_inc(sums_done, 1)

            def products(g, par, k, first):
                if k == 0:
                    pe.wait_ge(vb_ready, g + 1)
                    if not first:
                        pe.wait_ge(nrm_ready, g)
                pe.wait_ge(p_ready, UNITS * g + (TILES - 1 - FULL + k) // 2 + 1)
                if k == FULL:
                    mm_(ps[:, 4, 0:N], vb[:, par, P * k:P * k + P], prob[par][:, TILES - 1, :], start=False, stop=True,
                        skip_group_check=True).then_inc(pv_done, 1)
                    return
                for b in range(NB):
                    mm_(ps[C * b:C * b + C, 4, 0:N], vb[:, par, P * k + C * b:P * k + C * b + C],
                        prob[par][:, FULL * b + k, :], start=(k == 0), stop=False, skip_group_check=True)

            def center2(g, banks=NORM_BANKS):
                pe.wait_ge(t1_ready, g + 1)
                if banks[0] == NORM_BANKS[0]:
                    pe.wait_ge(xl2_ready, g + 1)
                mm_(ps[:, banks[0], 0:N], c_("center"), at(t0, g), start=True, stop=True).then_inc(centered2, 1)

            def variance2(g, banks=NORM_BANKS):
                pe.wait_ge(sq2_ready, g + 1)
                if banks[1] == NORM_BANKS[1]:
                    pe.wait_ge(stat_ready, g + 1)
                mm_(ps[:, banks[1], 0:N], c_("mean"), sq2, start=True, stop=True).then_inc(var2_done, 1)

            def wx(g, banks=NORM_BANKS):
                pe.wait_ge(xl2_ready, g + 1 + CREDIT1)
                mm_(ps[:, banks[1], 0:N], c_("wT"), at(xl2, g), start=True, stop=True).then_inc(wx_done, 1)

            PRODUCTS_AT = (1, 2, 4, 5)

            def attend(g, par):
                since = g if isinstance(g, int) else G
                for u in range(UNITS):
                    scores(g, par, u)
                    if since > 0 and u in PRODUCTS_AT:
                        products(g - 1, 1 - par, PRODUCTS_AT.index(u), first=since == 1)
                    if since > 0 and u == 3:
                        sums(g - 1, 1 - par, first=since == 1)
                        tail_sums(g - 1, 1 - par)
                    if since > 1 and u == 4:
                        center2(g - 2)
                    if since > 2 and u == 5:
                        wx(g - 3)
                    if since > 1 and u == 6:
                        variance2(g - 2)

            pe.wait_ge(operands_in[0], 96)
            for step, first, end in ((center, 0, 2), (variance, 2, 3), (project_kq, 3, 5), (project_v, 5, UNITS)):
                step(PAIRS - 1)
                for u in range(first, end):
                    scores(0, 0, u)
            pe.wait_ge(v_ready, G + CREDIT)
            pe.wait_ge(es_ready, G + CREDIT)
            for g in range(1, 4):
                pe.wait_ge(operands_in[g % 2], 96 * (g // 2 + 1))
                attend(g, g % 2)
            with pe.Fori(2, PAIRS) as i:
                for par in range(2):
                    g = 2 * i + par
                    pe.wait_ge(operands_in[par], 96 * i + 96)
                    attend(g, par)
            products(G - 1, 1, 0, False)
            center2(G - 2, LAST_BANKS[G - 2])
            wx(G - 3)
            sums(G - 1, 1, False)
            tail_sums(G - 1, 1)
            variance2(G - 2, LAST_BANKS[G - 2])
            for k in range(1, FULL + 1):
                products(G - 1, 1, k, False)
            wx(G - 2, LAST_BANKS[G - 2])
            center2(G - 1, LAST_BANKS[G - 1])
            variance2(G - 1, LAST_BANKS[G - 1])
            wx(G - 1, LAST_BANKS[G - 1])

            pe.wait_ge(bn_c, 3)
            mm_(ps[:, 5, 0:2], c_("avg4"), mm, start=True, stop=True).then_inc(bn_pe, 1)
            pe.wait_ge(bn_c, 6)
            mm_(ps[:, 6, 0:P], c_("w"), diag[:, :], start=True, stop=True).then_inc(bn_pe, 1)
            pe.wait_ge(wsc_ready, 1)

            def steps(base, sweep, count):
                with pe.Fori(0, count // UNROLL) as i:
                    for k, bank in enumerate(BANKS):
                        s = UNROLL * i + k
                        if k == 0:
                            pe.wait_ge(start_ok, sweep + 1)
                        for h in range(2):
                            pe.wait_ge(y_ok[h], base + s + 1)
                            mm_(ps[:, 4 * h + bank, 0:HALF], wsc[:, :],
                                xl2[:, 4 * h:4 * h + 4, bass.ds(NC * s, NC)],
                                start=True, stop=False)
                        for h in range(2):
                            pe.wait_ge(y_ok[h], base + s + CREDIT)
                            mm_(ps[:, 4 * h + bank, 0:HALF], c_("vT"),
                                yb[:, bass.ds(s, 1), 4 * h:4 * h + 4, :].rearrange("p o g c -> p (o g c)"),
                                start=False, stop=True).then_inc(pre[h], 1)

            for sweep in range(2):
                steps(L * sweep, sweep, L)
            pe.wait_ge(cmp_c, 6)
            mm_(ps[0:1, 7, 0:1], okc, c_("ones")[:, 0:1], start=True, stop=True).then_inc(cmp_pe, 1)
            pe.wait_ge(flag_ok, 1)
            with pe.If(pe.value_load(flag[0:1, 0:1], min_val=0, max_val=1) != 0):
                with pe.Fori(0, NC - 1) as k:
                    steps(2 * L + L * k, k + 2, L)



def _blocks(a, n):
    r, c = a.shape
    m = np.zeros((n * r, n * c), a.dtype)
    for k in range(n):
        m[k * r:k * r + r, k * c:k * c + c] = a
    return m


def _constants(i):
    f = np.float32
    m = np.zeros((P, ALL_W), f)

    def put(name, a):
        o, w = COLUMNS[name]
        a = np.asarray(a)
        assert a.shape[1] == w, name
        m[0:a.shape[0], o:o + w] = a

    put("ident", np.eye(P, dtype=f))
    for name, a in (("al", i["L0_conv_A_learned"]), ("alT", i["L0_conv_A_learned"].T), ("intraT", i["L0_conv_A_intra"].T),
                    ("interT", i["L0_conv_A_inter"].T), ("flatT", i["L0_conv_A_flat"].T)):
        put(name, _blocks(a, TT))
    bn = np.ones((4, P, 3), f)
    bn[:, :, 0] = np.tile(i["L0_conv_bn_gc"], (1, NB))
    for j, name in enumerate(("bn_b1", "bn_b2", "bn_b3", "bn_b4")):
        bn[:, C * j:C * j + C, 1] = np.tile(i["L0_conv_" + name], (1, NB))
    for b in range(NB):
        for j, name in enumerate(("bn_t1", "bn_t2", "bn_p3")):
            bn[:, C * b + CB * j:C * b + CB * j + CB, 2] = i["L0_conv_" + name]
    for k, name in enumerate(("bn_g", "bn_b", "bn_m", "bn_v")):
        put(name, bn[k])
    keep = np.ones((P, 3), f)
    keep[np.arange(P) % C >= 3 * CB, 2] = 0
    put("keep", keep)
    put("pass", 1 - keep)
    r = np.arange(P)[:, None] % RB
    put("not_first", np.where(np.isin(r, (1, 2)), -1, 0).astype(f))
    put("third", np.where(r == 2, -1, 0).astype(f))
    put("gamma", np.tile(i["L1_ffn_gamma"], NB)[:, None])
    put("beta", np.tile(i["L1_ffn_beta"], NB)[:, None])
    put("eps", np.full((P, 1), EPS, f))
    put("ones", np.ones((P, C), f))
    in_tail = (np.arange(P)[:, None] % C >= C - TAIL).astype(f)
    put("tail_ones", in_tail * _blocks(np.ones((C, C), f), NB))

    mix = np.zeros((2, NB, CH, NB, C), f)
    branch = np.zeros((P, BR, NB, CB), f)
    taps = np.zeros((len(OUTER), NB, CB, 2, NB, BR, CB), f)
    middle = np.zeros((BR, NB, CB, NB, BR, CB), f)
    for b in range(NB):
        mix[:, b, :, b] = i["L0_conv_Wgc"].T.reshape(2, CH, C)
        for j in range(BR):
            branch[C * b:C * b + C, j, b] = i[f"L0_conv_Wb{j + 1}"].T
        for j, name in enumerate(("Wt1", "Wt2")):
            w = i["L0_conv_" + name]
            for k, d in enumerate(OUTER):
                taps[k, b, :, j, b, j] = w[:, :, K // 2 + d].T
            middle[j, b, :, b, j] = w[:, :, K // 2].T
        for j in (2, 3):
            middle[j, b, :, b, j] = np.eye(CB, dtype=f)
    put("mix", mix.reshape(P, P))
    put("branch", branch.reshape(P, P))
    put("taps", taps.reshape(P, 2 * P))
    put("middle", middle.reshape(P, P))
    mean = np.full((C, C), 1 / C, f)
    put("mean", _blocks(mean, NB))
    put("center", _blocks(np.eye(C, dtype=f) - mean, NB))
    put("rotT", _blocks(i["L1_attn_rotation_params"].reshape(C, C).T, NB))
    put("entT", _blocks(i["L1_attn_entangle_params"].reshape(C, C).T, NB))
    put("wqT", _blocks(i["L1_attn_Wq"].T, NB))
    put("wkT", _blocks(i["L1_attn_Wk"].T, NB))
    put("wvT", _blocks(i["L1_attn_Wv"].T, NB))
    put("sel", _blocks(np.full((C, RB), -0.5, f), NB))
    put("wT", _blocks(i["L1_ffn_W"].T, NB))
    put("w", _blocks(i["L1_ffn_W"], NB))
    put("vT", _blocks(i["L1_ffn_V"].T, NB))
    put("avg4", np.tile(np.eye(C, dtype=f) / NB, (NB, NB)))
    return m


def kernel(**inputs):
    import concourse.bacc as bacc
    from concourse.bass_utils import run_bass_kernel_spmd

    i = {k: np.asarray(v) for k, v in inputs.items()}
    x = i["x"]
    by_token = x.reshape(G, NB, 2, CH, TT, MT).transpose(0, 5, 4, 2, 1, 3)
    arrays = {"x_tok": np.ascontiguousarray(by_token).reshape(G, MT, TT * P), "x": np.ascontiguousarray(x).reshape(G, P, N),
              "consts": _constants(i)}
    nc = bacc.Bacc("TRN2", target_bir_lowering=False, num_devices=1)
    args = [nc.dram_tensor(k, a.shape, F32, kind="ExternalInput").ap() for k, a in arrays.items()]
    out = nc.dram_tensor("out", (G, P, N), F32, kind="ExternalOutput").ap()
    build(nc, *args, out)
    got = run_bass_kernel_spmd(nc, [arrays], core_ids=[0]).results[0]["out"]
    return got.reshape(B, C, T, V)
```
